# Optimizing a Trainium2 kernel written in Bass

```python
import numpy as np
import jax
import jax.numpy as jnp

def _softmax(x, axis=-1):
    return jax.nn.softmax(x, axis=axis)

def _gelu(x):
    return jax.nn.gelu(x, approximate=True)

def _silu(x):
    return jax.nn.silu(x)

def _sigmoid(x):
    return jax.nn.sigmoid(x)

def _layernorm(x, axis=-1, eps=1e-05):
    m = jnp.mean(x, axis=axis, keepdims=True)
    v = jnp.var(x, axis=axis, keepdims=True)
    return (x - m) / jnp.sqrt(v + eps)

def _scatter_add(tgt, idx, src, axis=0):
    return tgt.at[idx].add(src)

def _segment_sum(src, seg, n):
    return jax.ops.segment_sum(src, seg, n)
kernel_name = 'mk_decoder_postln_d1_seqx_r8_719112'

def setup_inputs(seed: int=0):
    np.random.seed(seed)
    _w = jnp.asarray

    def _rec_inputs():
        import jax
        import jax.numpy as jnp
        _rk = jax.random.key(seed)
        x = 7.22e-05 + 1 * jax.random.normal(jax.random.fold_in(_rk, 1), (32, 64, 128), jnp.float32)
        _lenS = 64 - jax.random.randint(jax.random.fold_in(_rk, 7), (32,), 0, max(1, 64 // 4) + 1, jnp.int32)
        _lenS2 = 64 - jax.random.randint(jax.random.fold_in(_rk, 8), (32,), 0, max(1, 64 // 4) + 1, jnp.int32)
        _ctx_768P = jax.random.normal(jax.random.fold_in(_rk, 11), (32, 16, 96), jnp.float32)
        _ctx_768c = jax.random.dirichlet(jax.random.fold_in(_rk, 511), 0.3 * jnp.ones((16,), jnp.float32), (32, 64))
        _ctx_768t = jnp.einsum('bsk,bkd->bsd', _ctx_768c, _ctx_768P)
        _ctx_768t = _ctx_768t * jax.lax.rsqrt(jnp.mean(jnp.square(_ctx_768t)) + 1e-12) * 0.953939
        ctx_768 = 2.09791e-05 + 1.00001 * (_ctx_768t + 0.3 * jax.random.normal(jax.random.fold_in(_rk, 611), (32, 64, 96), jnp.float32))
        return (x, ctx_768)
    x, ctx_768 = _rec_inputs()

    def _L0_attn_setup():
        import jax, jax.numpy as jnp
        import numpy as np
        B, L, D = (4, 256, 128)
        S = 512
        DV = 128
        key = jax.random.key(seed)
        k1, k2, k3 = jax.random.split(key, 3)
        return {'inputs': jax.random.normal(k1, (B, L, D), dtype=jnp.float32), 'key_param_tokens': jax.random.normal(k2, (S, D), dtype=jnp.float32), 'value_param_tokens': jax.random.normal(k3, (S, DV), dtype=jnp.float32)}
    _L0_attn_all = _L0_attn_setup()
    _L0_attn_in = {k: v for k, v in _L0_attn_all.items() if k in ('key_param_tokens', 'value_param_tokens')}
    del _L0_attn_all

    def _L0_xattn_setup():
        import jax, jax.numpy as jnp
        import numpy as np
        HEADS = 16
        DIM_HEAD = 64
        key = jax.random.key(seed)
        ks = jax.random.split(key, 7)
        B, Nq, Dq = (4, 256, 128)
        Nk, Dc = (128, 96)
        inner = HEADS * DIM_HEAD
        sq = 1.0 / np.sqrt(Dq)
        sc = 1.0 / np.sqrt(Dc)
        si = 1.0 / np.sqrt(inner)
        return {'x': jax.random.normal(ks[0], (B, Nq, Dq), dtype=jnp.float32), 'context': jax.random.normal(ks[1], (B, Nk, Dc), dtype=jnp.float32), 'Wq': jax.random.normal(ks[2], (Dq, inner), dtype=jnp.float32) * sq, 'Wk': jax.random.normal(ks[3], (Dc, inner), dtype=jnp.float32) * sc, 'Wv': jax.random.normal(ks[4], (Dc, inner), dtype=jnp.float32) * sc, 'Wo': jax.random.normal(ks[5], (inner, Dq), dtype=jnp.float32) * si, 'bo': jax.random.normal(ks[6], (Dq,), dtype=jnp.float32) * 0.01}
    _L0_xattn_all = _L0_xattn_setup()
    _L0_xattn_in = {k: v for k, v in _L0_xattn_all.items() if k in ('Wq', 'Wk', 'Wv', 'Wo', 'bo')}
    del _L0_xattn_all

    def _L0_ffn_setup():
        import jax, jax.numpy as jnp
        import numpy as np
        B, S, D, F, E = (4, 256, 128, 512, 8)
        key = jax.random.key(seed)
        ks = jax.random.split(key, 7)
        s1 = 1.0 / np.sqrt(D)
        s2 = 1.0 / np.sqrt(F)
        x = jax.random.normal(ks[0], (B, S, D), dtype=jnp.float32)
        W1 = jax.random.uniform(ks[1], (E, D, F), jnp.float32, -s1, s1)
        b1 = jax.random.uniform(ks[2], (E, F), jnp.float32, -s1, s1)
        W2 = jax.random.uniform(ks[3], (E, F, D), jnp.float32, -s2, s2)
        b2 = jax.random.uniform(ks[4], (E, D), jnp.float32, -s2, s2)
        Wr = jax.random.uniform(ks[5], (D, E), jnp.float32, -s1, s1)
        br = jax.random.uniform(ks[6], (E,), jnp.float32, -s1, s1)
        return {'x': x, 'W1': W1, 'b1': b1, 'W2': W2, 'b2': b2, 'Wr': Wr, 'br': br}
    _L0_ffn_all = _L0_ffn_setup()
    _L0_ffn_in = {k: v for k, v in _L0_ffn_all.items() if k in ('W1', 'b1', 'W2', 'b2', 'Wr', 'br')}
    del _L0_ffn_all
    return {'x': x, 'ctx_768': ctx_768, 'L0_attn_key_param_tokens': _L0_attn_in['key_param_tokens'], 'L0_attn_value_param_tokens': _L0_attn_in['value_param_tokens'], 'L0_xattn_Wq': _L0_xattn_in['Wq'], 'L0_xattn_Wk': _L0_xattn_in['Wk'], 'L0_xattn_Wv': _L0_xattn_in['Wv'], 'L0_xattn_Wo': _L0_xattn_in['Wo'], 'L0_xattn_bo': _L0_xattn_in['bo'], 'L0_ffn_W1': _L0_ffn_in['W1'], 'L0_ffn_b1': _L0_ffn_in['b1'], 'L0_ffn_W2': _L0_ffn_in['W2'], 'L0_ffn_b2': _L0_ffn_in['b2'], 'L0_ffn_Wr': _L0_ffn_in['Wr'], 'L0_ffn_br': _L0_ffn_in['br']}

def reference(x, ctx_768, L0_attn_key_param_tokens, L0_attn_value_param_tokens, L0_xattn_Wq, L0_xattn_Wk, L0_xattn_Wv, L0_xattn_Wo, L0_xattn_bo, L0_ffn_W1, L0_ffn_b1, L0_ffn_W2, L0_ffn_b2, L0_ffn_Wr, L0_ffn_br):
    import jax
    import jax.numpy as jnp

    def _L0_attn_ref(inputs, key_param_tokens, value_param_tokens):
        import jax, jax.numpy as jnp
        import numpy as np
        B, L, D = (4, 256, 128)
        S = 512
        DV = 128
        scores = jnp.einsum('bld,sd->bls', inputs, key_param_tokens)
        g = jax.nn.gelu(scores, approximate=False)
        l2 = jnp.linalg.norm(g, axis=-1, keepdims=True)
        w = g / l2 * jnp.sqrt(jnp.asarray(g.shape[-1], g.dtype))
        return jnp.einsum('bls,sv->blv', w, value_param_tokens)

    def _L0_xattn_ref(x, context, Wq, Wk, Wv, Wo, bo):
        import jax, jax.numpy as jnp
        import numpy as np
        HEADS = 16
        DIM_HEAD = 64
        B, Nq, _ = x.shape
        Nk = context.shape[1]
        h, dh = (HEADS, DIM_HEAD)
        q = (x @ Wq).reshape(B, Nq, h, dh)
        k = (context @ Wk).reshape(B, Nk, h, dh)
        v = (context @ Wv).reshape(B, Nk, h, dh)
        scale = 1.0 / jnp.sqrt(jnp.asarray(dh, dtype=x.dtype))
        scores = jnp.einsum('bqhd,bkhd->bhqk', q, k) * scale
        attn = jax.nn.softmax(scores, axis=-1)
        out = jnp.einsum('bhqk,bkhd->bqhd', attn, v).reshape(B, Nq, h * dh)
        return out @ Wo + bo

    def _L0_ffn_ref(x, W1, b1, W2, b2, Wr, br):
        import jax, jax.numpy as jnp
        import numpy as np
        B, S, D, F, E = (4, 256, 128, 512, 8)
        b, s, d = x.shape
        e = Wr.shape[1]
        logits = x @ Wr + br
        idx = jnp.argmax(logits, axis=-1)
        probs = jax.nn.softmax(logits, axis=-1)
        gates = jnp.take_along_axis(probs, idx[..., None], axis=-1)[..., 0]
        xf = x.reshape(-1, d)
        idxf = idx.reshape(-1)
        gf = gates.reshape(-1)
        out = jnp.zeros_like(xf)
        for ei in range(e):
            h = jax.nn.gelu(xf @ W1[ei] + b1[ei], approximate=False)
            y = h @ W2[ei] + b2[ei]
            mask = (idxf == ei).astype(xf.dtype)
            out = out + y * (gf * mask)[:, None]
        return out.reshape(b, s, d)
    x = _layernorm(x + _L0_attn_ref(x, L0_attn_key_param_tokens, L0_attn_value_param_tokens), axis=-1)
    x = _layernorm(x + _L0_xattn_ref(x, ctx_768, L0_xattn_Wq, L0_xattn_Wk, L0_xattn_Wv, L0_xattn_Wo, L0_xattn_bo), axis=-1)
    x = _layernorm(x + _L0_ffn_ref(x, L0_ffn_W1, L0_ffn_b1, L0_ffn_W2, L0_ffn_b2, L0_ffn_Wr, L0_ffn_br), axis=-1)
    return x

_drawn_inputs = setup_inputs


def setup_inputs(seed=0):
    import zlib

    import numpy as np

    out = dict(_drawn_inputs(seed))
    spreads = {}
    factors = {'L0_xattn_bo': 5.602, 'L0_ffn_b1': 8.0, 'L0_ffn_b2': 8.0, 'L0_ffn_br': 3.843}
    for name, (base, spread) in spreads.items():
        noise = np.random.default_rng([zlib.crc32(name.encode()), seed]).standard_normal(out[name].shape)
        drawn = base * np.exp(spread * noise) if base else spread * noise
        out[name] = jnp.asarray(drawn.astype(out[name].dtype))
    for name, factor in factors.items():
        out[name] = (out[name] * factor).astype(out[name].dtype)
    return out
```

```python
from contextlib import ExitStack

import concourse.bass as bass
from concourse import mybir

ALU = mybir.AluOpType
ACT = mybir.ActivationFunctionType
F32 = mybir.dt.float32
F32R = mybir.dt.float32r
BF16 = mybir.dt.bfloat16
I32 = mybir.dt.int32
U32 = mybir.dt.uint32
AX = mybir.AxisListType

P = 128
EPS = 1e-5


def build_program(nc, x, ctx, key, value, wq, wk, wv, wo, bo, w1, b1, w2, b2, wr, br, out):
    B, L, D = x.shape
    C = ctx.shape[2]
    S = key.shape[0]
    INNER = wq.shape[1]
    DH = 64
    H = INNER // DH
    HP = H // 2
    E, _, F = w1.shape
    T = B * L
    NT = T // P
    SC = S // P
    FC = F // P
    NB = T // 512
    CB = T // 256
    assert D == P and L == DH and H * DH == INNER and T % 512 == 0
    TILES = -(-(NT + E - 1) // 4) * 4
    REGION = T + P
    SPARE = TILES - NT
    ROW = D + 4
    GATE, TOKEN = D, D + 1
    EW = F + FC + D
    SCALE = 1.0 / 8.0

    xf = x.rearrange("b s d -> (b s) d")
    cf = ctx.rearrange("b s c -> (b s) c")
    of = out.rearrange("b s d -> (b s) d")
    routed = nc.dram_tensor("routed_rows", [E * REGION + SPARE * P, ROW], F32).ap()

    es = ExitStack()
    with es:
        def sb(name, shape, dt=F32):
            return es.enter_context(nc.sbuf_tensor(name, shape, dt))

        def pb(name, shape):
            return es.enter_context(nc.psum_tensor(name, shape, F32))

        def sem(name):
            return es.enter_context(nc.semaphore(name))

        ident = sb("ident", [P, P])
        ones = sb("ones", [P, 1])
        ones_b = sb("ones_b", [P, P], BF16)
        before_b = sb("before_b", [P, P], BF16)
        minus_half = sb("minus_half", [P, 4])
        eps = sb("eps", [P, 4])
        expert_no = sb("expert_no", [P, E])
        region_base = sb("region_base", [P, E])
        token_no = sb("token_no", [P, NT], I32)
        tile_no = sb("tile_no", [1, TILES, E])
        tile_row = sb("tile_row", [1, TILES])
        le_expert = sb("le_expert", [1, E, E])
        pad_row = sb("pad_row", [P, ROW])
        bo_all = sb("bo_all", [P, D])
        br_all = sb("br_all", [P, E])
        wr_sb = sb("wr_sb", [P, E])
        key_in = sb("key_in", [P, SC, D])
        value_in = sb("value_in", [P, SC, D])
        key_hi = sb("key_hi", [P, S], F32R)
        key_lo = sb("key_lo", [P, S], F32R)
        a_hi = sb("a_hi", [C, 2, HP, D], F32R)
        a_lo = sb("a_lo", [C, 2, HP, D], F32R)
        b_sb = sb("b_sb", [C, 2, HP, D])
        ew_all = sb("ew_all", [P, E, EW])
        w2_all = sb("w2_all", [P, E, FC, D])
        b1_in = sb("b1_in", [E * FC, P])
        x1b_all = sb("x1b_all", [P, NT, D])
        x1t_all = sb("x1t_all", [P, T])

        z_all = sb("z_all", [P, 2, 2, 2, HP, D])
        zf = z_all[:, :, :, :, :, :].rearrange("p a b c e d -> p (a b c e d)")
        wq_in = zf[:, 0:1024]
        wk_in = zf[0:C, 1024:2048]
        wv_in = zf[0:C, 2048:3072]
        wo_in = zf[:, 3072:4096].rearrange("p (c n) -> p c n", n=D)
        wqt = zf[:, 4096:5120].rearrange("p (c n) -> p c n", n=D)
        wkt = zf[:, 5120:5888].rearrange("p (c n) -> p c n", n=C)
        wvt = zf[:, 5888:6656].rearrange("p (c n) -> p c n", n=C)

        kp_all = sb("kp_all", [P, 2, H, 256])
        kf = kp_all[:, :, :, :].rearrange("p a h t -> p (a h t)")
        g_sb = kf[:, 0:4096].rearrange("p (a c t) -> p a c t", a=2, c=SC)
        sq_sb = kf[:, 4096:6144].rearrange("p (c t) -> p c t", c=SC)
        ss_sb = kf[:, 6144:8192].rearrange("p (a c t) -> p a c t", a=2, c=2)

        x_in = sb("x_in", [P, NB, 4, D])
        x_hi = sb("x_hi", [P, 512], F32R)
        x_lo = sb("x_lo", [P, 512], F32R)
        ssv = sb("ssv", [P, 4])
        inv = sb("inv", [P, 4])
        r1 = sb("r1", [P, 4, D])
        st1 = sb("st1", [P, 4, 6])
        mv1 = sb("mv1", [P, 4, 2])
        ve1 = sb("ve1", [P, 4])
        rs1 = sb("rs1", [P, 4])
        x1 = sb("x1", [P, 2, 4, D])

        ctx_in = sb("ctx_in", [P, 2, 2, C])
        ctxt = sb("ctxt", [C, 2, 256])
        ctxt_hi = sb("ctxt_hi", [C, 2, 256], F32R)
        ctxt_lo = sb("ctxt_lo", [C, 2, 256], F32R)
        x1t = sb("x1t", [P, 2, P])
        smax = sb("smax", [P, H])
        ps_sb = sb("ps_sb", [P, H, L])
        pe_sb = sb("pe_sb", [P, H, L])
        psum_l = sb("psum_l", [P, H])
        pinv = sb("pinv", [P, H])
        pn_sb = sb("pn_sb", [P, H, L])
        pt_sb = sb("pt_sb", [P, HP, P])
        r2 = sb("r2", [P, D])
        st2 = sb("st2", [P, 6])
        mv2 = sb("mv2", [P, 2])
        ve2 = sb("ve2", [P, 1])
        rs2 = sb("rs2", [P, 1])
        row = sb("row", [P, 2, ROW])
        x2t = sb("x2t", [P, P])
        lg = sb("lg", [P, E])
        lmax = sb("lmax", [P, 8])
        lidx = sb("lidx", [P, 8], U32)
        lidf = sb("lidf", [P, 1])
        ld = sb("ld", [P, E])
        lexp = sb("lexp", [P, E])
        lsum = sb("lsum", [P, 1])
        oh_b = sb("oh_b", [P, E], BF16)
        seen_b = sb("seen_b", [P, E], BF16)
        place = sb("place", [P, E])
        placed = sb("placed", [P, E])
        posf = sb("posf", [P, 1])
        posi = sb("posi", [P, 2], I32)

        n_up = sb("n_up", [1, E])
        n_int = sb("n_int", [1, E], I32)
        n_sh = sb("n_sh", [1, E], I32)
        tiles_e = sb("tiles_e", [1, E])
        tl_mul = sb("tl_mul", [1, E, E])
        tl_end = sb("tl_end", [1, E])
        tl_skip = sb("tl_skip", [1, E])
        past = sb("past", [1, TILES, E])
        past_n = sb("past_n", [1, TILES])
        skip = sb("skip", [1, TILES, E])
        skip_n = sb("skip_n", [1, TILES])
        expert_of = sb("expert_of", [1, TILES], I32)
        row_of = sb("row_of", [1, TILES], I32)
        pad_at = sb("pad_at", [1, E], I32)

        xs = sb("xs", [P, 4, ROW])
        xst = sb("xst", [P, 2, P])
        ew = x_in[:, :, :, :].rearrange("p a c d -> p (a c d)")[:, 0:2 * EW].rearrange("p (a n) -> p a n", a=2)
        ht = ps_sb[:, :, :].rearrange("p h k -> p (h k)").rearrange("p (a c t) -> p a c t", a=2, c=FC)
        yb = sb("yb", [P, D])
        r3 = sb("r3", [P, D])
        st3 = sb("st3", [P, 6])
        mv3 = sb("mv3", [P, 2])
        ve3 = sb("ve3", [P, 1])
        rs3 = sb("rs3", [P, 1])
        ot = sb("ot", [P, 4, D])

        b01 = pb("b01", [P, 1024])
        b23 = pb("b23", [P, 1024])
        b4 = pb("b4", [P, 512])
        b5 = pb("b5", [P, 512])
        b6 = pb("b6", [P, 512])
        b7 = pb("b7", [P, 512])
        bank = [b01[:, 0:512], b01[:, 512:1024], b23[:, 0:512], b23[:, 512:1024],
                b4[:, :], b5[:, :], b6[:, :], b7[:, :]]
        s_ps = b01[:, :].rearrange("p (h k) -> p h k", k=L)
        pt_ps = b23[:, :].rearrange("p (c q) -> p c q", q=P)

        key_in_ok, value_in_ok, ctx_in_ok = sem("key_in_ok"), sem("value_in_ok"), [sem("ctx_in_ok0"), sem("ctx_in_ok1")]
        x_in_ok = [sem(f"x_in_ok{n}") for n in range(NB)]
        wqk_in_ok, wvo_in_ok, small_in_ok = sem("wqk_in_ok"), sem("wvo_in_ok"), sem("small_in_ok")
        experts_in_ok = sem("experts_in_ok")
        const_ok, seen_ok = sem("const_ok"), sem("seen_ok")
        keyt_ps, key_hi_ok, key_lo_ok = sem("keyt_ps"), sem("key_hi_ok"), sem("key_lo_ok")
        xt_ps, x_hi_ok, x_lo_ok = sem("xt_ps"), sem("x_hi_ok"), sem("x_lo_ok")
        sc_ps, gelu_ok, sq_ok = sem("sc_ps"), sem("gelu_ok"), sem("sq_ok")
        sqsum_ok, o1_ps, ss_ps, ssv_ok, inv_ok = sem("sqsum_ok"), sem("o1_ps"), sem("ss_ps"), sem("ssv_ok"), sem("inv_ok")
        r1_ok, st1_ok, mv1_ok, ve1_ok, rs1_ok = sem("r1_ok"), sem("st1_ok"), sem("mv1_ok"), sem("ve1_ok"), sem("rs1_ok")
        x1_ok, x1b_ok, x1t_ps, x1t_all_ok = sem("x1_ok"), sem("x1b_ok"), sem("x1t_ps"), sem("x1t_all_ok")
        wt_ps, wt_ok, ab_ps, a_hi_ok, a_lo_ok, b_ok = (sem("wt_ps"), sem("wt_ok"), sem("ab_ps"), sem("a_hi_ok"),
                                                         sem("a_lo_ok"), sem("b_ok"))
        b1t_ps, b1t_ok = sem("b1t_ps"), sem("b1t_ok")
        ctxt_ps, ctxt_ok, ctxt_hi_ok, ctxt_lo_ok = sem("ctxt_ps"), sem("ctxt_ok"), sem("ctxt_hi_ok"), sem("ctxt_lo_ok")
        kz_ps, kz_ok = sem("kz_ps"), sem("kz_ok")
        x1t_ok, s_ready, max_ok, sub_ok, exp_ok, sum_ok, pinv_ok, pn_ok = (
            sem("x1t_ok"), sem("s_ready"), sem("max_ok"), sem("sub_ok"), sem("exp_ok"), sem("sum_ok"),
            sem("pinv_ok"), sem("pn_ok"))
        pt_ready, pt_ok, o2_ps = sem("pt_ready"), sem("pt_ok"), sem("o2_ps")
        r2_ok, st2_ok, mv2_ok, ve2_ok, rs2_ok, x2_ok = (sem("r2_ok"), sem("st2_ok"), sem("mv2_ok"), sem("ve2_ok"),
                                                          sem("rs2_ok"), sem("x2_ok"))
        x2t_ps, x2t_ok, lg_ps, lg_ok, lmax_ok, lidx_ok, lidf_ok, oh_ok, ld_ok, lsum_ok = (
            sem("x2t_ps"), sem("x2t_ok"), sem("lg_ps"), sem("lg_ok"), sem("lmax_ok"), sem("lidx_ok"),
            sem("lidf_ok"), sem("oh_ok"), sem("ld_ok"), sem("lsum_ok"))
        rank_ps, place_ok, seen_up, placed_ok, placed2, row_ok, pos_ok = (
            sem("rank_ps"), sem("place_ok"), sem("seen_up"), sem("placed_ok"), sem("placed2"), sem("row_ok"), sem("pos_ok"))
        scat_ok = [sem("scat_ok0"), sem("scat_ok1")]
        count_ps, tab, table_ok, pad_ok, spare_ok = sem("count_ps"), sem("tab"), sem("table_ok"), sem("pad_ok"), sem("spare_ok")
        xs_ok = [sem(f"xs_ok{n}") for n in range(4)]
        xst_ps, xst_ok, ew_ok, h_ps, h_ok, y_ps = (sem("xst_ps"), sem("xst_ok"), sem("ew_ok"), sem("h_ps"),
                                                     sem("h_ok"), sem("y_ps"))
        yb_ok, r3_ok, st3_ok, mv3_ok, ve3_ok, rs3_ok, o3_ok = (sem("yb_ok"), sem("r3_ok"), sem("st3_ok"),
                                                                 sem("mv3_ok"), sem("ve3_ok"), sem("rs3_ok"), sem("o3_ok"))
        out_ok = [sem(f"out_ok{n}") for n in range(4)]

        CONSTS = 12

        def wait(eng, s, n):
            if not isinstance(n, int) or n > 0:
                eng.wait_ge(s, n)

        def waits_apart(eng, *waits):
            counts = [n if isinstance(n, int) else eng.to_reg(n) for _, n in waits]
            eng.wait_ge(const_ok, 1)
            for (s, _), n in zip(waits, counts):
                wait(eng, s, n)

        block = es.enter_context(nc.Block())

        @block.sync
        def _(sp):
            sp.dma_start(key_in[:, :, :], key.rearrange("(c p) d -> p c d", p=P)).then_inc(key_in_ok, 16)
            for n in range(NB):
                sp.dma_start(x_in[:, n, :, :], xf[512 * n:512 * (n + 1), :].rearrange("(c p) d -> p c d", p=P)
                             ).then_inc(x_in_ok[n], 16)
                if n == 0:
                    sp.dma_start(value_in[:, :, :], value.rearrange("(c p) d -> p c d", p=P)).then_inc(value_in_ok, 16)
            sp.dma_start(bo_all[:, :], bo.partition_broadcast(P)).then_inc(small_in_ok, 16)
            sp.dma_start(br_all[:, :], br.partition_broadcast(P)).then_inc(small_in_ok, 16)
            sp.dma_start(wr_sb[:, :], wr).then_inc(small_in_ok, 16)
            sp.dma_start(b1_in[:, :], b1.rearrange("e (c p) -> (e c) p", p=P)).then_inc(small_in_ok, 16)
            sp.dma_start(wq_in, wq).then_inc(wqk_in_ok, 16)
            sp.dma_start(wk_in, wk).then_inc(wqk_in_ok, 16)
            sp.dma_start(wv_in, wv).then_inc(wvo_in_ok, 16)
            sp.dma_start(wo_in, wo.rearrange("(c p) n -> p c n", p=P)).then_inc(wvo_in_ok, 16)
            for n in range(2):
                sp.dma_start(ctx_in[:, n, :, :], cf[256 * n:256 * (n + 1), :].rearrange("(c p) d -> p c d", p=P)
                             ).then_inc(ctx_in_ok[n], 16)
            sp.dma_start(ew_all[:, :, 0:F], w1.rearrange("e d f -> d e f")).then_inc(experts_in_ok, 16)
            sp.dma_start(ew_all[:, :, F + FC:EW], b2.partition_broadcast(P)).then_inc(experts_in_ok, 16)
            sp.dma_start(w2_all[:, :, :, :], w2.rearrange("e (c p) d -> p e c d", p=P)).then_inc(experts_in_ok, 16)
            sp.wait_ge(const_ok, CONSTS)
            for n in range(SPARE):
                sp.dma_start(routed[E * REGION + P * n:E * REGION + P * (n + 1), :], pad_row[:, :]
                             ).then_inc(spare_ok, 16)

            def ctx_load(n, slot):
                sp.wait_ge(ctxt_ps, n - 1)
                sp.dma_start(ctx_in[:, slot, :, :],
                             cf[bass.ds(n * 256, 256), :].rearrange("(c p) d -> p c d", p=P)
                             ).then_inc(ctx_in_ok[slot], 16)

            with sp.Fori(0, (CB - 2) // 2) as i:
                ctx_load(2 * i + 2, 0)
                ctx_load(2 * i + 3, 1)

            sp.wait_ge(table_ok, 1)
            for e in range(E):
                at = sp.value_load(pad_at[0:1, e:e + 1], min_val=e * REGION, max_val=e * REGION + T)
                sp.dma_start(routed[bass.ds(at, P), :], pad_row[:, :]).then_inc(pad_ok, 16)
            sp.wait_ge(pad_ok, 16 * E)
            sp.wait_ge(spare_ok, 16 * SPARE)
            for n in range(2):
                sp.wait_ge(scat_ok[n], 16 * (NT // 2))

            def tile_load(t, slot):
                if isinstance(t, int) and t < 4:
                    at = sp.value_load(row_of[0:1, t:t + 1], min_val=0, max_val=E * REGION + (SPARE - 1) * P)
                else:
                    sp.wait_ge(o3_ok, t - 3)
                    at = sp.value_load(row_of[0:1, bass.ds(t, 1)], min_val=0, max_val=E * REGION + (SPARE - 1) * P)
                    sp.wait_ge(out_ok[slot], 4 * (t - slot))
                sp.dma_start(xs[:, slot, :], routed[bass.ds(at, P), :]).then_inc(xs_ok[slot], 16)

            for u in range(4):
                tile_load(u, u)
            with sp.Fori(1, TILES // 4) as i:
                for u in range(4):
                    tile_load(4 * i + u, u)
            for n in range(4):
                sp.wait_ge(out_ok[n], 16 * (TILES // 4))

        @block.gpsimd
        def _(pl):
            g = nc.gpsimd
            g.memset(ident[:, :], 0.0).then_inc(const_ok, 1)
            pl.wait_ge(const_ok, 1)
            g.affine_select(out=ident[:, :], in_=ident[:, :], compare_op=ALU.not_equal, fill=1.0, base=0,
                            pattern=[[-1, P]], channel_multiplier=1).then_inc(const_ok, 1)
            g.memset(ones[:, :], 1.0).then_inc(const_ok, 1)
            g.memset(minus_half[:, :], -0.5).then_inc(const_ok, 1)
            g.memset(ones_b[:, :], 1.0).then_inc(const_ok, 1)
            g.memset(pad_row[:, :], 0.0).then_inc(const_ok, 1)
            pl.wait_ge(const_ok, 6)
            g.affine_select(out=before_b[:, :], in_=ones_b[:, :], compare_op=ALU.is_gt, fill=0.0, base=0,
                            pattern=[[1, P]], channel_multiplier=-1).then_inc(const_ok, 1)
            g.iota(pad_row[:, TOKEN:TOKEN + 1].bitcast(I32), [[0, 1]], base=2 * T, channel_multiplier=0
                   ).then_inc(const_ok, 1)
            g.iota(token_no[:, :], [[P, NT]], base=0, channel_multiplier=1).then_inc(const_ok, 1)
            g.iota(expert_no[:, :], [[1, E]], base=0, channel_multiplier=0,
                   allow_small_or_imprecise_dtypes=True).then_inc(const_ok, 1)
            g.iota(region_base[:, :], [[REGION, E]], base=0, channel_multiplier=0,
                   allow_small_or_imprecise_dtypes=True).then_inc(const_ok, 1)
            g.memset(row[:, :, TOKEN + 1:ROW], 0.0).then_inc(const_ok, 1)
            g.iota(tile_no[:, :, :], [[1, TILES], [0, E]], base=0, channel_multiplier=0,
                   allow_small_or_imprecise_dtypes=True).then_inc(seen_ok, 1)
            g.iota(tile_row[:, :], [[P, TILES]], base=0, channel_multiplier=0,
                   allow_small_or_imprecise_dtypes=True).then_inc(seen_ok, 1)
            g.memset(le_expert[:, :, :], 1.0).then_inc(seen_ok, 1)
            g.memset(seen_b[:, :], 0.0).then_inc(seen_ok, 1)
            g.memset(eps[:, :], EPS).then_inc(seen_ok, 1)
            pl.wait_ge(seen_ok, 5)
            last_routed, last_token = pl.to_reg(E * REGION - 1), pl.to_reg(T - 1)
            g.affine_select(out=le_expert[:, :, :], in_=le_expert[:, :, :], compare_op=ALU.is_ge, fill=0.0, base=0,
                            pattern=[[1, E], [-1, E]], channel_multiplier=0).then_inc(seen_ok, 1)
            pl.wait_ge(small_in_ok, 64)
            for n in range(NB):
                pl.wait_ge(ssv_ok, n + 1)
                wait(pl, r1_ok, n)
                g.tensor_tensor(inv[:, :], ssv[:, :], minus_half[:, :], ALU.pow).then_inc(inv_ok, 1)
                pl.wait_ge(mv1_ok, n + 1)
                g.tensor_tensor(ve1[:, :], mv1[:, :, 1], eps[:, :], ALU.add).then_inc(ve1_ok, 1)
                pl.wait_ge(ve1_ok, n + 1)
                wait(pl, x1_ok, n)
                g.tensor_tensor(rs1[:, :], ve1[:, :], minus_half[:, :], ALU.pow).then_inc(rs1_ok, 1)
                pl.wait_ge(x1_ok, n + 1)
                g.tensor_tensor(x1b_all[:, 4 * n:4 * n + 4, :], x1[:, n % 2, :, :],
                                bo_all[:, :].unsqueeze(1).broadcast_to([P, 4, D]), ALU.add).then_inc(x1b_ok, 1)

            def x1t_copy(p, s):
                wait(pl, s_ready, p - 1)
                src = x1t_all[:, P * p:P * (p + 1)] if isinstance(p, int) else x1t_all[:, bass.ds(p * P, P)]
                g.tensor_copy(x1t[:, s % 2, :], src).then_inc(x1t_ok, 1)

            def rstd(p):
                pl.wait_ge(mv2_ok, p + 1)
                g.tensor_tensor(ve2[:, :], mv2[:, 1:2], eps[:, 0:1], ALU.add).then_inc(ve2_ok, 1)
                pl.wait_ge(ve2_ok, p + 1)
                g.tensor_tensor(rs2[:, :], ve2[:, :], minus_half[:, 0:1], ALU.pow).then_inc(rs2_ok, 1)

            def scatter(p, s):
                waits_apart(pl, (row_ok, p + 1), (pos_ok, p + 1))
                g.indirect_dma_start(out=routed,
                                     out_offset=bass.IndirectOffsetOnAxis(ap=posi[:, s % 2:s % 2 + 1].bitcast(U32), axis=0),
                                     in_=row[:, s % 2, :], in_offset=None, bounds_check=last_routed,
                                     oob_is_err=False).then_inc(scat_ok[s % 2], 16)

            def slot(p, s, first=False, last=False):
                if not last:
                    x1t_copy(p + 2, s)
                if not first:
                    rstd(p - 1)
                    if not (isinstance(p, int) and p < 2):
                        scatter(p - 2, s)

            pl.wait_ge(x1t_all_ok, NB)
            x1t_copy(0, 0)
            x1t_copy(1, 1)
            for s in range(4):
                slot(s, s, first=(s == 0))
            with pl.Fori(1, NT // 4 - 1) as i:
                for s in range(4):
                    slot(4 * i + s, s)
            for s in range(4):
                slot(NT - 4 + s, s, last=(s >= 2))
            rstd(NT - 1)
            scatter(NT - 2, 0)
            scatter(NT - 1, 1)

            def finish(t, u):
                pl.wait_ge(mv3_ok, t + 1)
                g.tensor_tensor(ve3[:, :], mv3[:, 1:2], eps[:, 0:1], ALU.add).then_inc(ve3_ok, 1)
                pl.wait_ge(ve3_ok, t + 1)
                g.tensor_tensor(rs3[:, :], ve3[:, :], minus_half[:, 0:1], ALU.pow).then_inc(rs3_ok, 1)
                waits_apart(pl, (o3_ok, t + 1))
                g.indirect_dma_start(out=of,
                                     out_offset=bass.IndirectOffsetOnAxis(ap=xs[:, u, TOKEN:TOKEN + 1].bitcast(U32), axis=0),
                                     in_=ot[:, u, :], in_offset=None, bounds_check=last_token,
                                     oob_is_err=False).then_inc(out_ok[u], 16)

            with pl.Fori(0, TILES // 4) as i:
                for u in range(4):
                    finish(4 * i + u, u)

        @block.tensor
        def _(pe):
            mm = nc.tensor.matmul
            pe.wait_ge(const_ok, 3)
            pe.wait_ge(key_in_ok, 16)
            for c in range(SC):
                t = nc.tensor.transpose(bank[0][:, P * c:P * (c + 1)], key_in[:, c, :], ident[:, :])
            t.then_inc(keyt_ps, 1)

            def x_transposes(n):
                pe.wait_ge(x_in_ok[n], 16)
                wait(pe, x_lo_ok, n)
                for c in range(4):
                    t = nc.tensor.transpose(bank[1][:, P * c:P * (c + 1)], x_in[:, n, c, :], ident[:, :])
                t.then_inc(xt_ps, 1)

            def scores(n):
                pe.wait_ge(x_lo_ok, n + 1)
                if n == 0:
                    pe.wait_ge(key_lo_ok, 1)
                for c in range(SC):
                    i = SC * n + c
                    wait(pe, gelu_ok, i - 1)
                    o = bank[2 + i % 2]
                    kh, kl = key_hi[:, P * c:P * (c + 1)], key_lo[:, P * c:P * (c + 1)]
                    mm(o, kh, x_hi[:, :], start=True, stop=False)
                    mm(o, kh, x_lo[:, :], start=False, stop=False)
                    mm(o, kl, x_hi[:, :], start=False, stop=True).then_inc(sc_ps, 1)

            def gather(n):
                pe.wait_ge(gelu_ok, SC * (n + 1))
                wait(pe, r1_ok, n - 1)
                if n == 0:
                    pe.wait_ge(value_in_ok, 16)
                for t in range(4):
                    for c in range(SC):
                        m = mm(bank[4 + n % 2][:, P * t:P * (t + 1)], g_sb[:, n % 2, c, P * t:P * (t + 1)],
                               value_in[:, c, :], start=(c == 0), stop=(c == SC - 1))
                m.then_inc(o1_ps, 1)
                pe.wait_ge(sqsum_ok, 2 * (n + 1))
                wait(pe, ssv_ok, n)
                for t in range(4):
                    for c in range(2):
                        m = mm(bank[6][:, t:t + 1], ss_sb[:, n % 2, c, P * t:P * (t + 1)], ones[:, :],
                               start=(c == 0), stop=(c == 1))
                m.then_inc(ss_ps, 1)

            def x1_transposes(n):
                pe.wait_ge(x1_ok, n + 1)
                wait(pe, x1t_all_ok, n)
                for c in range(4):
                    t = nc.tensor.transpose(bank[7][:, P * c:P * (c + 1)], x1[:, n % 2, c, :], ident[:, :])
                t.then_inc(x1t_ps, 1)

            for n in range(NB):
                x_transposes(n)
                if n >= 1:
                    gather(n - 1)
                scores(n)
                if n >= 2:
                    x1_transposes(n - 2)
            gather(NB - 1)

            pe.wait_ge(wqk_in_ok, 32)
            x1_transposes(NB - 2)
            for i in range(6):
                if i == 4:
                    pe.wait_ge(wvo_in_ok, 32)
                wait(pe, wt_ok, i - 1)
                if i == 1:
                    pe.wait_ge(x_lo_ok, NB)
                w, rows = ((wq_in, P), (wk_in, C), (wv_in, C))[i // 2]
                for c in range(4):
                    at = (4 * (i % 2) + c) * P
                    t = nc.tensor.transpose(bank[i % 2][:, P * c:P * c + rows], w[:, at:at + P], ident[0:rows, 0:rows])
                t.then_inc(wt_ps, 1)
            x1_done = False
            for what in range(2):
                pe.wait_ge(wt_ok, (4, 6)[what])
                for half in range(2):
                    for h2 in range(2):
                        i = 4 * what + 2 * half + h2
                        o = bank[2 + i % 4]
                        if i < 2:
                            pe.wait_ge(gelu_ok, SC * NB)
                        elif i < 4:
                            pe.wait_ge(r1_ok, NB)
                        else:
                            pe.wait_ge(a_lo_ok, i - 3)
                        for c in range(4):
                            hp = 4 * half + c
                            rows = slice(DH * h2, DH * (h2 + 1))
                            left = (wkt, wvt)[what][rows, hp, :]
                            right = (wqt, wo_in)[what][rows, hp, :]
                            m = mm(o[0:C, P * c:P * (c + 1)], left, right, start=True, stop=True)
                        m.then_inc(ab_ps, 1)
            x1_transposes(NB - 1)
            pe.wait_ge(small_in_ok, 64)
            pe.wait_ge(wt_ok, 6)
            nc.tensor.transpose(bank[0][:, 0:E * FC], b1_in[:, :], ident[0:E * FC, 0:E * FC]).then_inc(b1t_ps, 1)

            def ctx_transposes(n, slot, p=None):
                pe.wait_ge(ctx_in_ok[slot], 8 * (n - slot) + 16)
                wait(pe, ctxt_ok, n)
                if p is None:
                    pe.wait_ge(x1t_all_ok, NB)
                else:
                    wait(pe, place_ok, p - 1)
                for c in range(2):
                    t = nc.tensor.transpose(bank[7][0:C, P * c:P * (c + 1)], ctx_in[:, slot, c, :], ident[:, :])
                t.then_inc(ctxt_ps, 1)

            def keys(n, q, i):
                if i == 0:
                    pe.wait_ge(ctxt_lo_ok, n + 1)
                wait(pe, kz_ok, 16 * n + i - 1)
                for c in range(2):
                    h = 2 * i + c
                    o = bank[4 + i % 2][:, 256 * c:256 * (c + 1)]
                    ah, al = a_hi[:, h % 2, h // 2, :], a_lo[:, h % 2, h // 2, :]
                    mm(o, ah, ctxt_hi[:, q, :], start=True, stop=False)
                    mm(o, ah, ctxt_lo[:, q, :], start=False, stop=False)
                    m = mm(o, al, ctxt_hi[:, q, :], start=False, stop=True)
                m.then_inc(kz_ps, 1)

            def values(n, q, i):
                pair, b, half = i // 4, i // 2 % 2, i % 2
                wait(pe, kz_ok, 16 * n + 8 + i - 1)
                at = P * pair + L * b
                for h2 in range(2):
                    m = mm(bank[4 + i % 2][DH * h2:DH * (h2 + 1), :], ctxt[:, q, at:at + L],
                           b_sb[:, h2, 4 * half:4 * half + 4, :].rearrange("c a d -> c (a d)"), start=True, stop=True)
                m.then_inc(kz_ps, 1)

            def cross_scores(p, s):
                q, j = s // 2 % 2, s % 2
                pe.wait_ge(x1t_ok, p + 1)
                wait(pe, sub_ok, p)
                pe.wait_ge(kz_ok, 8 * (p - j) + 8)
                for half in range(2):
                    for b in range(2):
                        at = P * j + L * b
                        m = mm(bank[half][L * b:L * (b + 1), :].rearrange("q (h k) -> q h k", k=L),
                               x1t[:, s % 2, L * b:L * (b + 1)], kp_all[:, q, 8 * half:8 * half + 8, at:at + L],
                               start=True, stop=True)
                m.then_inc(s_ready, 1)

            def prob_transposes(p):
                pe.wait_ge(pn_ok, p + 1)
                wait(pe, pt_ok, p)
                for c in range(HP):
                    t = nc.tensor.transpose(pt_ps[:, c, :], pn_sb[:, 2 * c:2 * c + 2, :].rearrange("p a k -> p (a k)"),
                                            ident[:, :])
                t.then_inc(pt_ready, 1)

            def attend(p, s):
                q, j = s // 2 % 2, s % 2
                pe.wait_ge(pt_ok, p + 1)
                wait(pe, r2_ok, p)
                pe.wait_ge(kz_ok, 8 * (p - j) + 16)
                for c in range(HP):
                    for b in range(2):
                        m = mm(bank[6][L * b:L * (b + 1), 0:D], pt_sb[:, c, L * b:L * (b + 1)],
                               z_all[:, q, j, b, c, :], start=(c == 0), stop=(c == HP - 1))
                m.then_inc(o2_ps, 1)

            def x2_transpose(p, has_ctx):
                pe.wait_ge(x2_ok, p + 1)
                wait(pe, place_ok, p)
                if has_ctx is not None:
                    pe.wait_ge(ctxt_ok, has_ctx + 1)
                nc.tensor.transpose(bank[7][:, 0:P], row[:, p_slot(p), 0:D], ident[:, :]).then_inc(x2t_ps, 1)

            slot_of = [0]

            def p_slot(p):
                return slot_of[0]

            def router_logits(p):
                pe.wait_ge(x2t_ok, p + 1)
                mm(bank[7][:, 256:256 + E], x2t[:, :], wr_sb[:, :], start=True, stop=True).then_inc(lg_ps, 1)

            def ranks(p):
                pe.wait_ge(oh_ok, p + 1)
                wait(pe, seen_up, p)
                o = bank[7][:, 384:384 + E]
                mm(o, before_b[:, :], oh_b[:, :], start=True, stop=False)
                mm(o, ones_b[:, :], seen_b[:, :], start=False, stop=True).then_inc(rank_ps, 1)

            def slot(p, s, first=False, last=False):
                j = s % 2
                more = not (last and s >= 2)
                if not (last and s == 3):
                    cross_scores(p + 1, s + 1)
                with_ctx = None
                if j == 1 and not (last and s >= 1):
                    n = blk(p, j) + 2
                    with_ctx = n
                    ctx_transposes(n, (s // 2) % 2, p)
                n, q = blk(p, j) + 1, (s // 2 + 1) % 2
                kz = (keys, values)[j]
                if more:
                    for i in range(3):
                        kz(n, q, i)
                slot_of[0] = (s - 1) % 2
                if not first:
                    x2_transpose(p - 1, with_ctx)
                if more:
                    kz(n, q, 3)
                prob_transposes(p)
                if more:
                    kz(n, q, 4)
                if not first:
                    router_logits(p - 1)
                if more:
                    for i in range(5, 8):
                        kz(n, q, i)
                attend(p, s)
                if not first:
                    ranks(p - 1)

            def blk(p, j):
                if isinstance(p, int):
                    return p // 2
                return blk_of[0]

            blk_of = [None]

            pe.wait_ge(b1t_ok, 1)
            ctx_transposes(0, 0)
            ctx_transposes(1, 1)
            pe.wait_ge(b_ok, 4)
            pe.wait_ge(ssv_ok, NB)
            for i in range(8):
                keys(0, 0, i)
            for i in range(8):
                values(0, 0, i)
            cross_scores(0, 0)
            for s in range(4):
                slot(s, s, first=(s == 0))
            with pe.Fori(1, NT // 4 - 1) as i:
                for s in range(4):
                    blk_of[0] = 2 * i + s // 2
                    slot(4 * i + s, s)
            for s in range(4):
                slot(NT - 4 + s, s, last=True)
            slot_of[0] = 1
            x2_transpose(NT - 1, None)
            router_logits(NT - 1)
            ranks(NT - 1)
            pe.wait_ge(seen_up, NT)
            mm(bank[7][:, 384:384 + E], ones_b[:, :], seen_b[:, :], start=True, stop=True).then_inc(count_ps, 1)

            def tile_transpose(t, u):
                pe.wait_ge(xs_ok[u], 16 * (idx4(t, u) + 1))
                wait(pe, xst_ok, t - 1)
                nc.tensor.transpose(bank[u % 2][:, 0:P], xs[:, u, 0:D], ident[:, :]).then_inc(xst_ps, 1)

            def hidden(t, u):
                pe.wait_ge(xst_ok, t + 1)
                pe.wait_ge(ew_ok, t + 1)
                wait(pe, h_ok, FC * (t - 1))
                for c in range(FC):
                    m = mm(bank[2 + u % 2][:, P * c:P * (c + 1)], ew[:, u % 2, P * c:P * (c + 1)], xst[:, u % 2, :],
                           start=True, stop=True)
                m.then_inc(h_ps, 1)

            def project(t, u):
                wait(pe, yb_ok, t - 1)
                e = pe.value_load(expert_of[0:1, bass.ds(t, 1)], min_val=0, max_val=E - 1)
                pe.wait_ge(h_ok, FC * (t + 1))
                for c in range(FC):
                    m = mm(bank[4 + u % 2][:, 0:D], ht[:, u % 2, c, :], w2_all[:, bass.ds(e, 1), c, :],
                           start=(c == 0), stop=(c == FC - 1))
                m.then_inc(y_ps, 1)

            def idx4(t, u):
                return t // 4 if isinstance(t, int) else it4[0] + (0 if u < 4 else 1)

            it4 = [None]

            def tile_slot(t, u, first=False, last=False):
                if not last:
                    u1 = (u + 1) % 4
                    if isinstance(t, int):
                        tile_transpose(t + 1, u1)
                    else:
                        pe.wait_ge(xs_ok[u1], 16 * (it4[0] + 1 + (1 if u == 3 else 0)))
                        wait(pe, xst_ok, t)
                        nc.tensor.transpose(bank[u1 % 2][:, 0:P], xs[:, u1, 0:D], ident[:, :]).then_inc(xst_ps, 1)
                hidden(t, u)
                if not first:
                    project(t - 1, (u - 1) % 4)

            pe.wait_ge(table_ok, 1)
            pe.wait_ge(experts_in_ok, 48)
            tile_transpose(0, 0)
            for u in range(4):
                tile_slot(u, u, first=(u == 0))
            with pe.Fori(1, TILES // 4 - 1) as i:
                it4[0] = i
                for u in range(4):
                    tile_slot(4 * i + u, u)
            for u in range(4):
                tile_slot(TILES - 4 + u, u, last=(u == 3))
            project(TILES - 1, 3)

        @block.scalar
        def _(act):
            a = nc.scalar.activation
            for n in range(NB):
                act.wait_ge(xt_ps, n + 1)
                wait(act, sc_ps, SC * n)
                a(x_hi[:, :], bank[1], ACT.Copy).then_inc(x_hi_ok, 1)
                wait(act, o1_ps, n - 1)
                for c in range(SC + 1):
                    if c < SC:
                        act.wait_ge(sc_ps, SC * n + c + 1)
                        a(g_sb[:, n % 2, c, :], bank[2 + c % 2], ACT.Gelu).then_inc(gelu_ok, 1)
                    if c >= 1:
                        act.wait_ge(gelu_ok, SC * n + c)
                        wait(act, sqsum_ok, 2 * n)
                        a(sq_sb[:, c - 1, :], g_sb[:, n % 2, c - 1, :], ACT.Square).then_inc(sq_ok, 1)
                if n >= 2:
                    act.wait_ge(x1t_ps, n - 1)
                    a(x1t_all[:, 512 * (n - 2):512 * (n - 1)], bank[7], ACT.Copy).then_inc(x1t_all_ok, 1)

            act.wait_ge(x1t_ps, NB - 1)
            a(x1t_all[:, 512 * (NB - 2):512 * (NB - 1)], bank[7], ACT.Copy).then_inc(x1t_all_ok, 1)
            for i in range(6):
                act.wait_ge(wt_ps, i + 1)
                dst, rows = ((wqt, P), (wkt, C), (wvt, C))[i // 2]
                a(dst[:, 4 * (i % 2):4 * (i % 2) + 4, :],
                  bank[i % 2].rearrange("p (c n) -> p c n", n=P)[:, :, 0:rows], ACT.Copy).then_inc(wt_ok, 1)
            for i in range(8):
                act.wait_ge(ab_ps, i + 1)
                half, h2 = i // 2 % 2, i % 2
                src = bank[2 + i % 4][0:C, :].rearrange("c (a d) -> c a d", d=D)
                if i < 4:
                    a(a_hi[:, h2, 4 * half:4 * half + 4, :], src, ACT.Copy).then_inc(a_hi_ok, 1)
                else:
                    a(b_sb[:, h2, 4 * half:4 * half + 4, :], src, ACT.Copy).then_inc(b_ok, 1)
            act.wait_ge(x1t_ps, NB)
            a(x1t_all[:, 512 * (NB - 1):512 * NB], bank[7], ACT.Copy).then_inc(x1t_all_ok, 1)
            act.wait_ge(b1t_ps, 1)
            a(ew_all[:, :, F:F + FC], bank[0][:, 0:E * FC].rearrange("p (e c) -> p e c", c=FC), ACT.Copy
              ).then_inc(b1t_ok, 1)

            def ctx_copy(n, slot):
                act.wait_ge(ctxt_ps, n + 1)
                a(ctxt[:, slot, :], bank[7][0:C, 0:256], ACT.Copy).then_inc(ctxt_ok, 1)

            def kz_copy(n, q, k):
                act.wait_ge(kz_ps, 16 * n + k + 1)
                src = bank[4 + k % 2]
                if k < 8:
                    dst = kp_all[:, q, 2 * k:2 * k + 2, :]
                    src = src.rearrange("p (c t) -> p c t", t=256)
                else:
                    i = k - 8
                    pair, b, half = i // 4, i // 2 % 2, i % 2
                    dst = z_all[:, q, pair, b, 4 * half:4 * half + 4, :]
                    src = src.rearrange("p (c t) -> p c t", t=D)
                a(dst, src, ACT.Copy).then_inc(kz_ok, 1)

            def exps(p):
                act.wait_ge(sub_ok, p + 1)
                wait(act, pn_ok, p)
                a(pe_sb[:, :, :], ps_sb[:, :, :], ACT.Exp, scale=SCALE).then_inc(exp_ok, 1)

            def gate_exp(p):
                act.wait_ge(ld_ok, p + 1)
                wait(act, row_ok, p)
                a(lexp[:, :], ld[:, :], ACT.Exp, accum_out=lsum[:, :]).then_inc(lsum_ok, 1)

            def prob_copy(p):
                act.wait_ge(pt_ready, p + 1)
                a(pt_sb[:, :, :], pt_ps, ACT.Copy).then_inc(pt_ok, 1)

            def x2t_copy(p):
                act.wait_ge(x2t_ps, p + 1)
                a(x2t[:, :], bank[7][:, 0:P], ACT.Copy).then_inc(x2t_ok, 1)

            def slot(p, s, n, first=False, last=False):
                j, q = s % 2, (s // 2 + 1) % 2
                more = not (last and s >= 2)
                if j == 1 and not (last and s >= 1):
                    ctx_copy(n + 1, (s // 2) % 2)
                if more:
                    for k in range(2):
                        kz_copy(n, q, 8 * j + k)
                if not (isinstance(p, int) and p < 2):
                    gate_exp(p - 2)
                if more and j == 0:
                    kz_copy(n, q, 2)
                if not (last and s == 3):
                    exps(p + 1)
                if more and j == 1:
                    kz_copy(n, q, 8 + 2)
                if not first:
                    x2t_copy(p - 1)
                if more:
                    kz_copy(n, q, 8 * j + 3)
                prob_copy(p)
                if more:
                    for k in range(4, 8):
                        kz_copy(n, q, 8 * j + k)

            ctx_copy(0, 0)
            ctx_copy(1, 1)
            for k in range(16):
                kz_copy(0, 0, k)
            exps(0)
            for s in range(4):
                slot(s, s, s // 2 + 1, first=(s == 0))
            with act.Fori(1, NT // 4 - 1) as i:
                for s in range(4):
                    slot(4 * i + s, s, 2 * i + s // 2 + 1)
            for s in range(4):
                slot(NT - 4 + s, s, (NT - 4 + s) // 2 + 1, last=True)
            gate_exp(NT - 2)
            x2t_copy(NT - 1)
            gate_exp(NT - 1)

            def tile_copy(t, u):
                act.wait_ge(xst_ps, t + 1)
                wait(act, h_ps, t - 1)
                a(xst[:, u % 2, :], bank[u % 2][:, 0:P], ACT.Copy).then_inc(xst_ok, 1)

            def gelus(t, u):
                act.wait_ge(h_ps, t + 1)
                wait(act, y_ps, t - 1)
                for c in range(FC):
                    a(ht[:, u % 2, c, :], bank[2 + u % 2][:, P * c:P * (c + 1)], ACT.Gelu,
                      bias=ew[:, u % 2, F + c:F + c + 1]).then_inc(h_ok, 1)

            tile_copy(0, 0)
            for u in range(4):
                tile_copy(u + 1, u + 1)
                gelus(u, u)
            with act.Fori(1, TILES // 4 - 1) as i:
                for u in range(4):
                    tile_copy(4 * i + u + 1, u + 1)
                    gelus(4 * i + u, u)
            for u in range(4):
                if u < 3:
                    tile_copy(TILES - 4 + u + 1, u + 1)
                gelus(TILES - 4 + u, u)

        @block.vector
        def _(dve):
            v = nc.vector
            dve.wait_ge(keyt_ps, 1)
            v.tensor_copy(key_hi[:, :], bank[0]).then_inc(key_hi_ok, 1)
            dve.wait_ge(key_hi_ok, 1)
            v.tensor_tensor(key_lo[:, :], bank[0], key_hi[:, :].bitcast(F32), ALU.subtract).then_inc(key_lo_ok, 1)

            def split_x(n):
                dve.wait_ge(x_hi_ok, n + 1)
                wait(dve, sc_ps, SC * n)
                v.tensor_tensor(x_lo[:, :], bank[1], x_hi[:, :].bitcast(F32), ALU.subtract).then_inc(x_lo_ok, 1)

            def norm1(n):
                dve.wait_ge(ss_ps, n + 1)
                wait(dve, inv_ok, n)
                v.tensor_scalar(ssv[:, :], bank[6][:, 0:4], 1.0 / S, None, ALU.mult).then_inc(ssv_ok, 1)
                dve.wait_ge(inv_ok, n + 1)
                dve.wait_ge(o1_ps, n + 1)
                wait(dve, x1_ok, n)
                for t in range(4):
                    m = v.scalar_tensor_tensor(r1[:, t, :], bank[4 + n % 2][:, P * t:P * (t + 1)], inv[:, t:t + 1],
                                               x_in[:, n, t, :], ALU.mult, ALU.add)
                m.then_inc(r1_ok, 1)
                dve.wait_ge(r1_ok, n + 1)
                for t in range(4):
                    m = v.bn_stats(st1[:, t, :], r1[:, t, :])
                m.then_inc(st1_ok, 1)
                dve.wait_ge(st1_ok, n + 1)
                wait(dve, ve1_ok, n)
                for t in range(4):
                    m = v.bn_aggr(mv1[:, t, :], st1[:, t, :])
                m.then_inc(mv1_ok, 1)
                dve.wait_ge(rs1_ok, n + 1)
                wait(dve, x1t_ps, n - 1)
                wait(dve, x1b_ok, n - 1)
                for t in range(4):
                    m = v.tensor_scalar(x1[:, n % 2, t, :], r1[:, t, :], mv1[:, t, 0:1], rs1[:, t:t + 1],
                                        ALU.subtract, ALU.mult)
                m.then_inc(x1_ok, 1)

            for n in range(NB):
                split_x(n)
                if n >= 1:
                    norm1(n - 1)
                wait(dve, ss_ps, n - 1)
                for c in range(2):
                    dve.wait_ge(sq_ok, SC * n + 2 * c + 2)
                    v.tensor_tensor(ss_sb[:, n % 2, c, :], sq_sb[:, 2 * c, :], sq_sb[:, 2 * c + 1, :], ALU.add
                                    ).then_inc(sqsum_ok, 1)
            norm1(NB - 1)
            for i in range(4):
                dve.wait_ge(a_hi_ok, i + 1)
                half, h2 = i // 2, i % 2
                v.tensor_tensor(a_lo[:, h2, 4 * half:4 * half + 4, :],
                                bank[2 + i][0:C, :].rearrange("c (a d) -> c a d", d=D),
                                a_hi[:, h2, 4 * half:4 * half + 4, :].bitcast(F32), ALU.subtract).then_inc(a_lo_ok, 1)

            def split_ctx(n, slot):
                dve.wait_ge(ctxt_ok, n + 1)
                wait(dve, kz_ps, 16 * (n - 1) - 8)
                v.tensor_copy(ctxt_hi[:, slot, :], ctxt[:, slot, :]).then_inc(ctxt_hi_ok, 1)
                dve.wait_ge(ctxt_hi_ok, n + 1)
                v.tensor_tensor(ctxt_lo[:, slot, :], ctxt[:, slot, :], ctxt_hi[:, slot, :].bitcast(F32), ALU.subtract
                                ).then_inc(ctxt_lo_ok, 1)

            def heads(t):
                return t[:, :].unsqueeze(2).broadcast_to([P, H, L])

            def maxes(p):
                dve.wait_ge(s_ready, p + 1)
                v.reduce_max(smax[:, :], s_ps, AX.X).then_inc(max_ok, 1)

            def subtract_max(p):
                dve.wait_ge(max_ok, p + 1)
                wait(dve, exp_ok, p)
                v.tensor_tensor(ps_sb[:, :, :], s_ps, heads(smax), ALU.subtract).then_inc(sub_ok, 1)

            def normalise(p):
                dve.wait_ge(exp_ok, p + 1)
                v.reduce_sum(psum_l[:, :], pe_sb[:, :, :], AX.X).then_inc(sum_ok, 1)
                dve.wait_ge(sum_ok, p + 1)
                v.reciprocal(pinv[:, :], psum_l[:, :]).then_inc(pinv_ok, 1)
                dve.wait_ge(pinv_ok, p + 1)
                wait(dve, pt_ready, p)
                v.tensor_tensor(pn_sb[:, :, :], pe_sb[:, :, :], heads(pinv), ALU.mult).then_inc(pn_ok, 1)

            def at(tensor, p):
                return tensor[:, p, :] if isinstance(p, int) else tensor[:, bass.ds(p, 1), :]

            def stats2(p):
                dve.wait_ge(o2_ps, p + 1)
                v.tensor_tensor(r2[:, :], bank[6][:, 0:D], at(x1b_all, p), ALU.add).then_inc(r2_ok, 1)
                dve.wait_ge(r2_ok, p + 1)
                v.bn_stats(st2[:, :], r2[:, :]).then_inc(st2_ok, 1)
                waits_apart(dve, (x2_ok, p), (st2_ok, p + 1))
                v.bn_aggr(mv2[:, :], st2[:, :]).then_inc(mv2_ok, 1)

            def norm2(p, s):
                dve.wait_ge(rs2_ok, p + 1)
                if not (isinstance(p, int) and p < 2):
                    dve.wait_ge(scat_ok[s % 2], 8 * (p - s % 2))
                v.tensor_scalar(row[:, s % 2, 0:D], r2[:, :], mv2[:, 0:1], rs2[:, :], ALU.subtract, ALU.mult
                                ).then_inc(x2_ok, 1)

            def choose(p, s):
                dve.wait_ge(lg_ps, p + 1)
                v.tensor_tensor(lg[:, :], bank[7][:, 256:256 + E], br_all[:, :], ALU.add).then_inc(lg_ok, 1)
                waits_apart(dve, (lg_ok, p + 1))
                v.max(lmax[:, :], lg[:, :]).then_inc(lmax_ok, 1)
                waits_apart(dve, (lmax_ok, p + 1))
                v.max_index(lidx[:, :], lmax[:, :], lg[:, :]).then_inc(lidx_ok, 1)
                v.tensor_scalar(ld[:, :], lg[:, :], lmax[:, 0:1], None, ALU.subtract).then_inc(ld_ok, 1)
                dve.wait_ge(lidx_ok, p + 1)
                v.tensor_copy(lidf[:, :], lidx[:, 0:1]).then_inc(lidf_ok, 1)
                dve.wait_ge(lidf_ok, p + 1)
                wait(dve, rank_ps, p)
                v.tensor_scalar(oh_b[:, :], expert_no[:, :], lidf[:, :], None, ALU.is_equal).then_inc(oh_ok, 1)

            def finish_row(p, s):
                dve.wait_ge(rank_ps, p + 1)
                v.tensor_tensor(place[:, :], bank[7][:, 384:384 + E], region_base[:, :], ALU.add
                                ).then_inc(place_ok, 1)
                v.tensor_tensor(seen_b[:, :], seen_b[:, :], oh_b[:, :], ALU.add).then_inc(seen_up, 1)
                dve.wait_ge(place_ok, p + 1)
                v.tensor_tensor(placed[:, :], place[:, :], oh_b[:, :], ALU.mult).then_inc(placed_ok, 1)
                dve.wait_ge(lsum_ok, p + 1)
                v.reciprocal(row[:, s % 2, GATE:GATE + 1], lsum[:, :])
                src = token_no[:, p:p + 1] if isinstance(p, int) else token_no[:, bass.ds(p, 1)]
                v.tensor_copy(row[:, s % 2, TOKEN:TOKEN + 1].bitcast(I32), src).then_inc(row_ok, 1)
                dve.wait_ge(placed_ok, p + 1)
                v.reduce_sum(posf[:, :], placed[:, :], AX.X).then_inc(placed2, 1)
                dve.wait_ge(placed2, p + 1)
                v.tensor_copy(posi[:, s % 2:s % 2 + 1], posf[:, :]).then_inc(pos_ok, 1)

            def slot(p, s, n, first=False, last=False):
                if not first:
                    stats2(p - 1)
                    if not (isinstance(p, int) and p < 2):
                        finish_row(p - 2, s)
                if not (last and s == 3):
                    maxes(p + 1)
                    subtract_max(p + 1)
                if not first:
                    norm2(p - 1, s - 1)
                if s % 2 == 1 and not (last and s >= 1):
                    split_ctx(n + 1, (s // 2) % 2)
                if not (last and s == 3):
                    normalise(p + 1)
                if not first:
                    choose(p - 1, s - 1)

            split_ctx(0, 0)
            split_ctx(1, 1)
            maxes(0)
            subtract_max(0)
            normalise(0)
            for s in range(4):
                slot(s, s, s // 2 + 1, first=(s == 0))
            with dve.Fori(1, NT // 4 - 1) as i:
                for s in range(4):
                    slot(4 * i + s, s, 2 * i + s // 2 + 1)
            for s in range(4):
                slot(NT - 4 + s, s, (NT - 4 + s) // 2 + 1, last=True)
            stats2(NT - 1)
            finish_row(NT - 2, 0)
            norm2(NT - 1, 1)
            choose(NT - 1, 1)
            finish_row(NT - 1, 1)

            steps = [0]

            def step(ins):
                steps[0] += 1
                ins.then_inc(tab, 1)
                dve.wait_ge(tab, steps[0])

            dve.wait_ge(count_ps, 1)
            dve.wait_ge(seen_ok, 6)
            counts = bank[7][0:1, 384:384 + E]
            step(v.tensor_tensor(pad_at[:, :], counts, region_base[0:1, :], ALU.add))
            step(v.tensor_scalar(n_int[:, :], counts, float(P - 1), None, ALU.add))
            step(v.tensor_scalar(n_sh[:, :], n_int[:, :], 7, None, ALU.logical_shift_right))
            step(v.tensor_copy(tiles_e[:, :], n_sh[:, :]))
            step(v.tensor_scalar(tl_skip[:, :], tiles_e[:, :], -float(P), float(REGION), ALU.mult, ALU.add))
            step(v.tensor_tensor(tl_mul[:, :, :], tiles_e[:, :].unsqueeze(1).broadcast_to([1, E, E]),
                                 le_expert[:, :, :], ALU.mult))
            step(v.reduce_sum(tl_end[:, :], tl_mul[:, :, :], AX.X))
            wide = [1, TILES, E]
            step(v.tensor_tensor(past[:, :, :], tl_end[:, :].unsqueeze(1).broadcast_to(wide), tile_no[:, :, :],
                                 ALU.is_le))
            step(v.reduce_sum(past_n[:, :], past[:, :, :], AX.X))
            step(v.tensor_scalar(expert_of[:, :], past_n[:, :], float(E - 1), None, ALU.min))
            step(v.tensor_tensor(skip[:, :, :], past[:, :, :], tl_skip[:, :].unsqueeze(1).broadcast_to(wide),
                                 ALU.mult))
            step(v.reduce_sum(skip_n[:, :], skip[:, :, :], AX.X))
            v.tensor_tensor(row_of[:, :], skip_n[:, :], tile_row[:, :], ALU.add).then_inc(table_ok, 1)
            dve.wait_ge(table_ok, 1)
            dve.wait_ge(experts_in_ok, 48)
            dve.wait_ge(b1t_ok, 1)

            def expert_copy(t, u):
                e = dve.value_load(expert_of[0:1, bass.ds(t, 1)], min_val=0, max_val=E - 1)
                wait(dve, h_ok, FC * (t - 1))
                v.tensor_copy(ew[:, u % 2, :], ew_all[:, bass.ds(e, 1), :]).then_inc(ew_ok, 1)

            def stats3(t, u):
                dve.wait_ge(y_ps, t + 1)
                dve.wait_ge(ew_ok, t + 1)
                v.tensor_tensor(yb[:, :], bank[4 + u % 2][:, 0:D], ew[:, u % 2, F + FC:EW], ALU.add
                                ).then_inc(yb_ok, 1)
                dve.wait_ge(yb_ok, t + 1)
                dve.wait_ge(xs_ok[u], 16 * quarter(t, u))
                v.scalar_tensor_tensor(r3[:, :], yb[:, :], xs[:, u, GATE:GATE + 1], xs[:, u, 0:D], ALU.mult, ALU.add
                                       ).then_inc(r3_ok, 1)
                dve.wait_ge(r3_ok, t + 1)
                v.bn_stats(st3[:, :], r3[:, :]).then_inc(st3_ok, 1)
                waits_apart(dve, (o3_ok, t), (st3_ok, t + 1))
                v.bn_aggr(mv3[:, :], st3[:, :]).then_inc(mv3_ok, 1)

            def norm3(t, u):
                dve.wait_ge(rs3_ok, t + 1)
                if not (isinstance(t, int) and t < 4):
                    dve.wait_ge(out_ok[u], 16 * (quarter(t, u) - 1))
                v.tensor_scalar(ot[:, u, :], r3[:, :], mv3[:, 0:1], rs3[:, :], ALU.subtract, ALU.mult
                                ).then_inc(o3_ok, 1)

            quarter_of = [None]

            def quarter(t, u):
                return t // 4 + 1 if isinstance(t, int) else quarter_of[0] + (0 if u == 3 else 1)

            def tile_slot(t, u, first=False, last=False):
                if not first:
                    stats3(t - 1, (u - 1) % 4)
                if not last:
                    expert_copy(t + 1, u + 1)
                if not first:
                    norm3(t - 1, (u - 1) % 4)

            expert_copy(0, 0)
            for u in range(4):
                tile_slot(u, u, first=(u == 0))
            with dve.Fori(1, TILES // 4 - 1) as i:
                quarter_of[0] = i
                for u in range(4):
                    tile_slot(4 * i + u, u)
            for u in range(4):
                tile_slot(TILES - 4 + u, u, last=(u == 3))
            stats3(TILES - 1, 3)
            norm3(TILES - 1, 3)


_INS = ["x", "ctx_768", "L0_attn_key_param_tokens", "L0_attn_value_param_tokens", "L0_xattn_Wq", "L0_xattn_Wk",
        "L0_xattn_Wv", "L0_xattn_Wo", "L0_xattn_bo", "L0_ffn_W1", "L0_ffn_b1", "L0_ffn_W2", "L0_ffn_b2",
        "L0_ffn_Wr", "L0_ffn_br"]


def kernel(**inputs):
    import numpy as np
    import concourse.bacc as bacc
    from concourse import mybir as mb
    from concourse.bass_utils import run_bass_kernel_spmd

    nc = bacc.Bacc("TRN2", target_bir_lowering=False, num_devices=1)
    arrays, args = {}, []
    for name in _INS:
        a = np.ascontiguousarray(inputs[name])
        arrays[f"in_{name}"] = a
        args.append(nc.dram_tensor(f"in_{name}", a.shape, mb.dt.from_np(a.dtype), kind="ExternalInput").ap())
    args.append(nc.dram_tensor("out", (32, 64, 128), mb.dt.float32, kind="ExternalOutput").ap())
    build_program(nc, *args)
    r = run_bass_kernel_spmd(nc, [arrays], core_ids=[0])
    return r.results[0]["out"]
```

```python
import math
from contextlib import ExitStack

import concourse.bass as bass
from concourse import mybir

ALU = mybir.AluOpType
ACT = mybir.ActivationFunctionType
F32 = mybir.dt.float32
F32R = mybir.dt.float32r
BF16 = mybir.dt.bfloat16
I32 = mybir.dt.int32
U32 = mybir.dt.uint32
AX = mybir.AxisListType

P = 128
EPS = 1e-5


def build_program(nc, x, ctx, key, value, wq, wk, wv, wo, bo, w1, b1, w2, b2, wr, br, out):
    B, L, D = x.shape
    C = ctx.shape[2]
    S = key.shape[0]
    INNER = wq.shape[1]
    DH = 64
    H = INNER // DH
    HP = H // 2
    E, _, F = w1.shape
    T = B * L
    NT = T // P
    SC = S // P
    FC = F // P
    NB = T // 512
    CB = T // 256
    assert D == P and L == DH and H * DH == INNER and T % 512 == 0
    U = 6
    TILES = -(-(NT + E - 1) // U) * U
    ROUNDS = TILES // U
    REGION = T + P
    SPARE = TILES - NT
    ROW = D + 4
    GATE, TOKEN = D, D + 1
    EW = F + FC + D
    SCALE = 1.0 / 8.0

    xf = x.rearrange("b s d -> (b s) d")
    cf = ctx.rearrange("b s c -> (b s) c")
    of = out.rearrange("b s d -> (b s) d")
    routed = nc.dram_tensor("routed_rows", [E * REGION + SPARE * P, ROW], F32).ap()

    es = ExitStack()
    with es:
        def sb(name, shape, dt=F32):
            return es.enter_context(nc.sbuf_tensor(name, shape, dt))

        def pb(name, shape):
            return es.enter_context(nc.psum_tensor(name, shape, F32))

        def sem(name):
            return es.enter_context(nc.semaphore(name))

        ident = sb("ident", [P, P])
        ones = sb("ones", [P, 1])
        ones_b = sb("ones_b", [P, P], BF16)
        before_b = sb("before_b", [P, P], BF16)
        minus_half = sb("minus_half", [P, 4])
        eps = sb("eps", [P, 4])
        expert_no = sb("expert_no", [P, E])
        region_base = sb("region_base", [P, E])
        token_no = sb("token_no", [P, NT], I32)
        tile_no = sb("tile_no", [1, TILES, E])
        tile_row = sb("tile_row", [1, TILES])
        le_expert = sb("le_expert", [1, E, E])
        pad_row = sb("pad_row", [P, ROW])
        bo_all = sb("bo_all", [P, D])
        br_all = sb("br_all", [P, E])
        wr_sb = sb("wr_sb", [P, E])
        key_in = sb("key_in", [P, SC, D])
        value_in = sb("value_in", [P, SC, D])
        key_hi = sb("key_hi", [P, S], F32R)
        key_lo = sb("key_lo", [P, S], F32R)
        a_hi = sb("a_hi", [C, 2, HP, D], F32R)
        a_lo = sb("a_lo", [C, 2, HP, D], F32R)
        b_sb = sb("b_sb", [C, 2, HP, D])
        ew_all = sb("ew_all", [P, E, EW])
        w2_all = sb("w2_all", [P, E, FC, D])
        b1_in = sb("b1_in", [E * FC, P])
        x1b_all = sb("x1b_all", [P, NT, D])
        x1t_all = sb("x1t_all", [P, T])

        z_all = sb("z_all", [P, 2, 2, 2, HP, D])
        zf = z_all[:, :, :, :, :, :].rearrange("p a b c e d -> p (a b c e d)")
        wq_in = zf[:, 0:1024]
        wk_in = zf[0:C, 1024:2048]
        wv_in = zf[0:C, 2048:3072]
        wo_in = zf[:, 3072:4096].rearrange("p (c n) -> p c n", n=D)
        wqt = zf[:, 4096:5120].rearrange("p (c n) -> p c n", n=D)
        wkt = zf[:, 5120:5888].rearrange("p (c n) -> p c n", n=C)
        wvt = zf[:, 5888:6656].rearrange("p (c n) -> p c n", n=C)

        kp_all = sb("kp_all", [P, 2, H, 256])
        kf = kp_all[:, :, :, :].rearrange("p a h t -> p (a h t)")
        g_sb = kf[:, 0:4096].rearrange("p (a c t) -> p a c t", a=2, c=SC)
        sq_sb = kf[:, 4096:6144].rearrange("p (c t) -> p c t", c=SC)
        ss_sb = kf[:, 6144:8192].rearrange("p (a c t) -> p a c t", a=2, c=2)

        x_in = sb("x_in", [P, NB, 4, D])
        x_hi = sb("x_hi", [P, 512], F32R)
        x_lo = sb("x_lo", [P, 512], F32R)
        ssv = sb("ssv", [P, 4])
        inv = sb("inv", [P, 4])
        r1 = sb("r1", [P, 4, D])
        st1 = sb("st1", [P, 4, 6])
        mv1 = sb("mv1", [P, 4, 2])
        ve1 = sb("ve1", [P, 4])
        rs1 = sb("rs1", [P, 4])
        x1 = sb("x1", [P, 2, 4, D])

        ctx_in = sb("ctx_in", [P, 2, 2, C])
        ctxt = sb("ctxt", [C, 2, 256])
        ctxt_hi = sb("ctxt_hi", [C, 2, 256], F32R)
        ctxt_lo = sb("ctxt_lo", [C, 2, 256], F32R)
        x1t = sb("x1t", [P, 2, P])
        smax = sb("smax", [P, H])
        ps_sb = sb("ps_sb", [P, H, L])
        pe_sb = sb("pe_sb", [P, H, L])
        psum_l = sb("psum_l", [P, H])
        pinv = sb("pinv", [P, H])
        pn_sb = sb("pn_sb", [P, H, L])
        pt_sb = sb("pt_sb", [P, HP, P])
        r2 = sb("r2", [P, D])
        st2 = sb("st2", [P, 6])
        mv2 = sb("mv2", [P, 2])
        ve2 = sb("ve2", [P, 1])
        rs2 = sb("rs2", [P, 1])
        row = sb("row", [P, 2, ROW])
        x2t = sb("x2t", [P, P])
        lg = sb("lg", [P, E])
        lmax = sb("lmax", [P, 8])
        lidx = sb("lidx", [P, 8], U32)
        lidf = sb("lidf", [P, 1])
        ld = sb("ld", [P, E])
        lexp = sb("lexp", [P, E])
        lsum = sb("lsum", [P, 1])
        oh_b = sb("oh_b", [P, E], BF16)
        seen_b = sb("seen_b", [P, E], BF16)
        place = sb("place", [P, E])
        placed = sb("placed", [P, E])
        posf = sb("posf", [P, 1])
        posi = sb("posi", [P, 2], I32)

        n_up = sb("n_up", [1, E])
        n_int = sb("n_int", [1, E], I32)
        n_sh = sb("n_sh", [1, E], I32)
        tiles_e = sb("tiles_e", [1, E])
        tl_mul = sb("tl_mul", [1, E, E])
        tl_end = sb("tl_end", [1, E])
        tl_skip = sb("tl_skip", [1, E])
        past = sb("past", [1, TILES, E])
        past_n = sb("past_n", [1, TILES])
        skip = sb("skip", [1, TILES, E])
        skip_n = sb("skip_n", [1, TILES])
        expert_of = sb("expert_of", [1, TILES], I32)
        row_of = sb("row_of", [1, TILES], I32)
        pad_at = sb("pad_at", [1, E], I32)

        taken = [0]

        def part(*shape):
            size = math.prod(shape)
            at, taken[0] = taken[0], taken[0] + size
            assert taken[0] <= 2 * H * 256
            flat = kf[:, at:at + size]
            if len(shape) == 1:
                return flat
            if len(shape) == 2:
                return flat.rearrange("p (a n) -> p a n", n=shape[1])
            return flat.rearrange("p (a c n) -> p a c n", c=shape[1], n=shape[2])

        xs = part(U, ROW)
        ew = part(U, EW)
        xst = part(2, P)
        ht = part(2, FC, P)
        yb = part(2, D)
        r3 = part(2, D)
        st3 = part(2, 6)
        mv3 = part(2, 2)
        rs3 = part(2, 1)
        ve3 = part(1)
        ot = part(U, D)

        b01 = pb("b01", [P, 1024])
        b23 = pb("b23", [P, 1024])
        b4 = pb("b4", [P, 512])
        b5 = pb("b5", [P, 512])
        b6 = pb("b6", [P, 512])
        b7 = pb("b7", [P, 512])
        bank = [b01[:, 0:512], b01[:, 512:1024], b23[:, 0:512], b23[:, 512:1024],
                b4[:, :], b5[:, :], b6[:, :], b7[:, :]]
        s_ps = b01[:, :].rearrange("p (h k) -> p h k", k=L)
        pt_ps = b23[:, :].rearrange("p (c q) -> p c q", q=P)

        key_in_ok, value_in_ok, ctx_in_ok = sem("key_in_ok"), sem("value_in_ok"), [sem("ctx_in_ok0"), sem("ctx_in_ok1")]
        x_in_ok = [sem(f"x_in_ok{n}") for n in range(NB)]
        wqk_in_ok, wvo_in_ok, small_in_ok = sem("wqk_in_ok"), sem("wvo_in_ok"), sem("small_in_ok")
        experts_in_ok = sem("experts_in_ok")
        const_ok, seen_ok = sem("const_ok"), sem("seen_ok")
        keyt_ps, key_hi_ok, key_lo_ok = sem("keyt_ps"), sem("key_hi_ok"), sem("key_lo_ok")
        xt_ps, x_hi_ok, x_lo_ok = sem("xt_ps"), sem("x_hi_ok"), sem("x_lo_ok")
        sc_ps, gelu_ok, sq_ok = sem("sc_ps"), sem("gelu_ok"), sem("sq_ok")
        sqsum_ok, o1_ps, ss_ps, ssv_ok, inv_ok = sem("sqsum_ok"), sem("o1_ps"), sem("ss_ps"), sem("ssv_ok"), sem("inv_ok")
        r1_ok, st1_ok, mv1_ok, ve1_ok, rs1_ok = sem("r1_ok"), sem("st1_ok"), sem("mv1_ok"), sem("ve1_ok"), sem("rs1_ok")
        x1_ok, x1b_ok, x1t_ps, x1t_all_ok = sem("x1_ok"), sem("x1b_ok"), sem("x1t_ps"), sem("x1t_all_ok")
        wt_ps, wt_ok, ab_ps, a_hi_ok, a_lo_ok, b_ok = (sem("wt_ps"), sem("wt_ok"), sem("ab_ps"), sem("a_hi_ok"),
                                                         sem("a_lo_ok"), sem("b_ok"))
        b1t_ps, b1t_ok = sem("b1t_ps"), sem("b1t_ok")
        ctxt_ps, ctxt_ok, ctxt_hi_ok, ctxt_lo_ok = sem("ctxt_ps"), sem("ctxt_ok"), sem("ctxt_hi_ok"), sem("ctxt_lo_ok")
        kz_ps, kz_ok = sem("kz_ps"), sem("kz_ok")
        x1t_ok, s_ready, max_ok, sub_ok, exp_ok, sum_ok, pinv_ok, pn_ok = (
            sem("x1t_ok"), sem("s_ready"), sem("max_ok"), sem("sub_ok"), sem("exp_ok"), sem("sum_ok"),
            sem("pinv_ok"), sem("pn_ok"))
        pt_ready, pt_ok, o2_ps = sem("pt_ready"), sem("pt_ok"), sem("o2_ps")
        r2_ok, st2_ok, mv2_ok, ve2_ok, rs2_ok, x2_ok = (sem("r2_ok"), sem("st2_ok"), sem("mv2_ok"), sem("ve2_ok"),
                                                          sem("rs2_ok"), sem("x2_ok"))
        x2t_ps, x2t_ok, lg_ps, lg_ok, lmax_ok, lidx_ok, lidf_ok, oh_ok, ld_ok, lsum_ok = (
            sem("x2t_ps"), sem("x2t_ok"), sem("lg_ps"), sem("lg_ok"), sem("lmax_ok"), sem("lidx_ok"),
            sem("lidf_ok"), sem("oh_ok"), sem("ld_ok"), sem("lsum_ok"))
        rank_ps, place_ok, seen_up, placed_ok, placed2, row_ok, pos_ok = (
            sem("rank_ps"), sem("place_ok"), sem("seen_up"), sem("placed_ok"), sem("placed2"), sem("row_ok"), sem("pos_ok"))
        scat_ok = [sem("scat_ok0"), sem("scat_ok1")]
        count_ps, tab, table_ok, pad_ok, spare_ok = sem("count_ps"), sem("tab"), sem("table_ok"), sem("pad_ok"), sem("spare_ok")
        xs_ok = [sem(f"xs_ok{n}") for n in range(U)]
        xst_ps, xst_ok, ew_ok, h_ps, h_ok, y_ps = (sem("xst_ps"), sem("xst_ok"), sem("ew_ok"), sem("h_ps"),
                                                     sem("h_ok"), sem("y_ps"))
        yb_ok, r3_ok, st3_ok, mv3_ok, ve3_ok, rs3_ok, o3_ok = (sem("yb_ok"), sem("r3_ok"), sem("st3_ok"),
                                                                 sem("mv3_ok"), sem("ve3_ok"), sem("rs3_ok"), sem("o3_ok"))
        out_ok = [sem(f"out_ok{n}") for n in range(U)]

        CONSTS = 12

        def wait(eng, s, n):
            if not isinstance(n, int) or n > 0:
                eng.wait_ge(s, n)

        def waits_apart(eng, *waits):
            counts = [n if isinstance(n, int) else eng.to_reg(n) for _, n in waits]
            eng.wait_ge(const_ok, 1)
            for (s, _), n in zip(waits, counts):
                wait(eng, s, n)

        def tiles(eng, slot):
            for u in range(U):
                slot(0, u)
            with eng.Fori(1, ROUNDS - 1) as i:
                for u in range(U):
                    slot(i, u)
            for u in range(U):
                slot(ROUNDS - 1, u)

        def ahead(i, u, n):
            if isinstance(i, int) and U * i + u + n >= TILES:
                return None
            return i + (u + n) // U, (u + n) % U

        block = es.enter_context(nc.Block())

        @block.sync
        def _(sp):
            sp.dma_start(key_in[:, :, :], key.rearrange("(c p) d -> p c d", p=P)).then_inc(key_in_ok, 16)
            for n in range(NB):
                sp.dma_start(x_in[:, n, :, :], xf[512 * n:512 * (n + 1), :].rearrange("(c p) d -> p c d", p=P)
                             ).then_inc(x_in_ok[n], 16)
                if n == 0:
                    sp.dma_start(value_in[:, :, :], value.rearrange("(c p) d -> p c d", p=P)).then_inc(value_in_ok, 16)
            sp.dma_start(bo_all[:, :], bo.partition_broadcast(P)).then_inc(small_in_ok, 16)
            sp.dma_start(br_all[:, :], br.partition_broadcast(P)).then_inc(small_in_ok, 16)
            sp.dma_start(wr_sb[:, :], wr).then_inc(small_in_ok, 16)
            sp.dma_start(b1_in[:, :], b1.rearrange("e (c p) -> (e c) p", p=P)).then_inc(small_in_ok, 16)
            sp.dma_start(wq_in, wq).then_inc(wqk_in_ok, 16)
            sp.dma_start(wk_in, wk).then_inc(wqk_in_ok, 16)
            sp.dma_start(wv_in, wv).then_inc(wvo_in_ok, 16)
            sp.dma_start(wo_in, wo.rearrange("(c p) n -> p c n", p=P)).then_inc(wvo_in_ok, 16)
            for n in range(2):
                sp.dma_start(ctx_in[:, n, :, :], cf[256 * n:256 * (n + 1), :].rearrange("(c p) d -> p c d", p=P)
                             ).then_inc(ctx_in_ok[n], 16)
            sp.dma_start(ew_all[:, :, 0:F], w1.rearrange("e d f -> d e f")).then_inc(experts_in_ok, 16)
            sp.dma_start(ew_all[:, :, F + FC:EW], b2.partition_broadcast(P)).then_inc(experts_in_ok, 16)
            sp.dma_start(w2_all[:, :, :, :], w2.rearrange("e (c p) d -> p e c d", p=P)).then_inc(experts_in_ok, 16)
            sp.wait_ge(const_ok, CONSTS)
            for n in range(SPARE):
                sp.dma_start(routed[E * REGION + P * n:E * REGION + P * (n + 1), :], pad_row[:, :]
                             ).then_inc(spare_ok, 16)

            def ctx_load(n, slot):
                sp.wait_ge(ctxt_ps, n - 1)
                sp.dma_start(ctx_in[:, slot, :, :],
                             cf[bass.ds(n * 256, 256), :].rearrange("(c p) d -> p c d", p=P)
                             ).then_inc(ctx_in_ok[slot], 16)

            with sp.Fori(0, (CB - 2) // 2) as i:
                ctx_load(2 * i + 2, 0)
                ctx_load(2 * i + 3, 1)

            sp.wait_ge(tab, 1)
            for e in range(E):
                at = sp.value_load(pad_at[0:1, e:e + 1], min_val=e * REGION, max_val=e * REGION + T)
                sp.dma_start(routed[bass.ds(at, P), :], pad_row[:, :]).then_inc(pad_ok, 16)
            sp.wait_ge(table_ok, 1)
            sp.wait_ge(pad_ok, 16 * E)
            sp.wait_ge(spare_ok, 16 * SPARE)
            for n in range(2):
                sp.wait_ge(scat_ok[n], 16 * (NT // 2))

            def tile_load(i, u):
                if not (isinstance(i, int) and i == 0):
                    sp.wait_ge(out_ok[u], 16 * i)
                at = sp.value_load(row_of[0:1, bass.ds(U * i + u, 1)], min_val=0,
                                   max_val=E * REGION + (SPARE - 1) * P)
                sp.dma_start(xs[:, u, :], routed[bass.ds(at, P), :]).then_inc(xs_ok[u], 16)

            tiles(sp, tile_load)
            for u in range(U):
                sp.wait_ge(out_ok[u], 16 * ROUNDS)

        @block.gpsimd
        def _(pl):
            g = nc.gpsimd
            g.memset(ident[:, :], 0.0).then_inc(const_ok, 1)
            pl.wait_ge(const_ok, 1)
            g.affine_select(out=ident[:, :], in_=ident[:, :], compare_op=ALU.not_equal, fill=1.0, base=0,
                            pattern=[[-1, P]], channel_multiplier=1).then_inc(const_ok, 1)
            g.memset(ones[:, :], 1.0).then_inc(const_ok, 1)
            g.memset(minus_half[:, :], -0.5).then_inc(const_ok, 1)
            g.memset(ones_b[:, :], 1.0).then_inc(const_ok, 1)
            g.memset(pad_row[:, :], 0.0).then_inc(const_ok, 1)
            pl.wait_ge(const_ok, 6)
            g.affine_select(out=before_b[:, :], in_=ones_b[:, :], compare_op=ALU.is_gt, fill=0.0, base=0,
                            pattern=[[1, P]], channel_multiplier=-1).then_inc(const_ok, 1)
            g.iota(pad_row[:, TOKEN:TOKEN + 1].bitcast(I32), [[0, 1]], base=2 * T, channel_multiplier=0
                   ).then_inc(const_ok, 1)
            g.iota(token_no[:, :], [[P, NT]], base=0, channel_multiplier=1).then_inc(const_ok, 1)
            g.iota(expert_no[:, :], [[1, E]], base=0, channel_multiplier=0,
                   allow_small_or_imprecise_dtypes=True).then_inc(const_ok, 1)
            g.iota(region_base[:, :], [[REGION, E]], base=0, channel_multiplier=0,
                   allow_small_or_imprecise_dtypes=True).then_inc(const_ok, 1)
            g.memset(row[:, :, TOKEN + 1:ROW], 0.0).then_inc(const_ok, 1)
            g.iota(tile_no[:, :, :], [[1, TILES], [0, E]], base=0, channel_multiplier=0,
                   allow_small_or_imprecise_dtypes=True).then_inc(seen_ok, 1)
            g.iota(tile_row[:, :], [[P, TILES]], base=0, channel_multiplier=0,
                   allow_small_or_imprecise_dtypes=True).then_inc(seen_ok, 1)
            g.memset(le_expert[:, :, :], 1.0).then_inc(seen_ok, 1)
            g.memset(seen_b[:, :], 0.0).then_inc(seen_ok, 1)
            g.memset(eps[:, :], EPS).then_inc(seen_ok, 1)
            pl.wait_ge(seen_ok, 5)
            last_routed, last_token = pl.to_reg(E * REGION - 1), pl.to_reg(T - 1)
            g.affine_select(out=le_expert[:, :, :], in_=le_expert[:, :, :], compare_op=ALU.is_ge, fill=0.0, base=0,
                            pattern=[[1, E], [-1, E]], channel_multiplier=0).then_inc(seen_ok, 1)
            pl.wait_ge(small_in_ok, 64)
            for n in range(NB):
                pl.wait_ge(ssv_ok, n + 1)
                wait(pl, r1_ok, n)
                g.tensor_tensor(inv[:, :], ssv[:, :], minus_half[:, :], ALU.pow).then_inc(inv_ok, 1)
                pl.wait_ge(mv1_ok, n + 1)
                g.tensor_tensor(ve1[:, :], mv1[:, :, 1], eps[:, :], ALU.add).then_inc(ve1_ok, 1)
                pl.wait_ge(ve1_ok, n + 1)
                wait(pl, x1_ok, n)
                g.tensor_tensor(rs1[:, :], ve1[:, :], minus_half[:, :], ALU.pow).then_inc(rs1_ok, 1)
                pl.wait_ge(x1_ok, n + 1)
                g.tensor_tensor(x1b_all[:, 4 * n:4 * n + 4, :], x1[:, n % 2, :, :],
                                bo_all[:, :].unsqueeze(1).broadcast_to([P, 4, D]), ALU.add).then_inc(x1b_ok, 1)

            def x1t_copy(p, s):
                wait(pl, s_ready, p - 1)
                src = x1t_all[:, P * p:P * (p + 1)] if isinstance(p, int) else x1t_all[:, bass.ds(p * P, P)]
                g.tensor_copy(x1t[:, s % 2, :], src).then_inc(x1t_ok, 1)

            def rstd(p):
                pl.wait_ge(mv2_ok, p + 1)
                g.tensor_tensor(ve2[:, :], mv2[:, 1:2], eps[:, 0:1], ALU.add).then_inc(ve2_ok, 1)
                pl.wait_ge(ve2_ok, p + 1)
                g.tensor_tensor(rs2[:, :], ve2[:, :], minus_half[:, 0:1], ALU.pow).then_inc(rs2_ok, 1)

            def scatter(p, s):
                waits_apart(pl, (row_ok, p + 1), (pos_ok, p + 1))
                g.indirect_dma_start(out=routed,
                                     out_offset=bass.IndirectOffsetOnAxis(ap=posi[:, s % 2:s % 2 + 1].bitcast(U32), axis=0),
                                     in_=row[:, s % 2, :], in_offset=None, bounds_check=last_routed,
                                     oob_is_err=False).then_inc(scat_ok[s % 2], 16)

            def slot(p, s, last=False):
                if not (isinstance(p, int) and p == 0):
                    scatter(p - 1, s - 1)
                rstd(p)
                if not (last and s >= 2):
                    x1t_copy(p + 2, s)

            pl.wait_ge(x1t_all_ok, NB)
            x1t_copy(0, 0)
            x1t_copy(1, 1)
            for s in range(4):
                slot(s, s)
            with pl.Fori(1, NT // 4 - 1) as i:
                for s in range(4):
                    slot(4 * i + s, s)
            for s in range(4):
                slot(NT - 4 + s, s, last=True)
            scatter(NT - 1, 1)

            def scatter_out(i, u):
                waits_apart(pl, (o3_ok, U * i + u + 1))
                g.indirect_dma_start(out=of,
                                     out_offset=bass.IndirectOffsetOnAxis(ap=xs[:, u, TOKEN:TOKEN + 1].bitcast(U32), axis=0),
                                     in_=ot[:, u, :], in_offset=None, bounds_check=last_token,
                                     oob_is_err=False).then_inc(out_ok[u], 16)

            def slot(i, u):
                if not (isinstance(i, int) and U * i + u == 0):
                    scatter_out(*((i, u - 1) if u else (i - 1, U - 1)))
                pl.wait_ge(mv3_ok, U * i + u + 1)
                wait(pl, o3_ok, U * i + u - 1)
                g.tensor_tensor(ve3[:, :], mv3[:, u % 2, 1:2], eps[:, 0:1], ALU.add).then_inc(ve3_ok, 1)
                pl.wait_ge(ve3_ok, U * i + u + 1)
                g.tensor_tensor(rs3[:, u % 2, :], ve3[:, :], minus_half[:, 0:1], ALU.pow).then_inc(rs3_ok, 1)

            tiles(pl, slot)
            scatter_out(ROUNDS - 1, U - 1)

        @block.tensor
        def _(pe):
            mm = nc.tensor.matmul
            pe.wait_ge(const_ok, 3)
            pe.wait_ge(key_in_ok, 16)
            for c in range(SC):
                t = nc.tensor.transpose(bank[0][:, P * c:P * (c + 1)], key_in[:, c, :], ident[:, :])
            t.then_inc(keyt_ps, 1)

            def x_transposes(n):
                pe.wait_ge(x_in_ok[n], 16)
                wait(pe, x_lo_ok, n)
                for c in range(4):
                    t = nc.tensor.transpose(bank[1][:, P * c:P * (c + 1)], x_in[:, n, c, :], ident[:, :])
                t.then_inc(xt_ps, 1)

            def scores(n):
                pe.wait_ge(x_lo_ok, n + 1)
                if n == 0:
                    pe.wait_ge(key_lo_ok, 1)
                for c in range(SC):
                    i = SC * n + c
                    wait(pe, gelu_ok, i - 1)
                    o = bank[2 + i % 2]
                    kh, kl = key_hi[:, P * c:P * (c + 1)], key_lo[:, P * c:P * (c + 1)]
                    mm(o, kh, x_hi[:, :], start=True, stop=False)
                    mm(o, kh, x_lo[:, :], start=False, stop=False)
                    mm(o, kl, x_hi[:, :], start=False, stop=True).then_inc(sc_ps, 1)

            def gather(n):
                pe.wait_ge(gelu_ok, SC * (n + 1))
                wait(pe, r1_ok, n - 1)
                if n == 0:
                    pe.wait_ge(value_in_ok, 16)
                for t in range(4):
                    for c in range(SC):
                        m = mm(bank[4 + n % 2][:, P * t:P * (t + 1)], g_sb[:, n % 2, c, P * t:P * (t + 1)],
                               value_in[:, c, :], start=(c == 0), stop=(c == SC - 1))
                m.then_inc(o1_ps, 1)
                pe.wait_ge(sqsum_ok, 2 * (n + 1))
                wait(pe, ssv_ok, n)
                for t in range(4):
                    for c in range(2):
                        m = mm(bank[6][:, t:t + 1], ss_sb[:, n % 2, c, P * t:P * (t + 1)], ones[:, :],
                               start=(c == 0), stop=(c == 1))
                m.then_inc(ss_ps, 1)

            def x1_transposes(n):
                pe.wait_ge(x1_ok, n + 1)
                wait(pe, x1t_all_ok, n)
                for c in range(4):
                    t = nc.tensor.transpose(bank[7][:, P * c:P * (c + 1)], x1[:, n % 2, c, :], ident[:, :])
                t.then_inc(x1t_ps, 1)

            for n in range(NB):
                x_transposes(n)
                if n >= 1:
                    gather(n - 1)
                scores(n)
                if n >= 2:
                    x1_transposes(n - 2)
            gather(NB - 1)

            pe.wait_ge(wqk_in_ok, 32)
            x1_transposes(NB - 2)
            for i in range(6):
                if i == 4:
                    pe.wait_ge(wvo_in_ok, 32)
                wait(pe, wt_ok, i - 1)
                if i == 1:
                    pe.wait_ge(x_lo_ok, NB)
                w, rows = ((wq_in, P), (wk_in, C), (wv_in, C))[i // 2]
                for c in range(4):
                    at = (4 * (i % 2) + c) * P
                    t = nc.tensor.transpose(bank[i % 2][:, P * c:P * c + rows], w[:, at:at + P], ident[0:rows, 0:rows])
                t.then_inc(wt_ps, 1)
            x1_done = False
            for what in range(2):
                pe.wait_ge(wt_ok, (4, 6)[what])
                for half in range(2):
                    for h2 in range(2):
                        i = 4 * what + 2 * half + h2
                        o = bank[2 + i % 4]
                        if i < 2:
                            pe.wait_ge(gelu_ok, SC * NB)
                        elif i < 4:
                            pe.wait_ge(r1_ok, NB)
                        else:
                            pe.wait_ge(a_lo_ok, i - 3)
                        for c in range(4):
                            hp = 4 * half + c
                            rows = slice(DH * h2, DH * (h2 + 1))
                            left = (wkt, wvt)[what][rows, hp, :]
                            right = (wqt, wo_in)[what][rows, hp, :]
                            m = mm(o[0:C, P * c:P * (c + 1)], left, right, start=True, stop=True)
                        m.then_inc(ab_ps, 1)
            x1_transposes(NB - 1)
            pe.wait_ge(small_in_ok, 64)
            pe.wait_ge(wt_ok, 6)
            nc.tensor.transpose(bank[0][:, 0:E * FC], b1_in[:, :], ident[0:E * FC, 0:E * FC]).then_inc(b1t_ps, 1)

            def ctx_transposes(n, slot, p=None):
                pe.wait_ge(ctx_in_ok[slot], 8 * (n - slot) + 16)
                wait(pe, ctxt_ok, n)
                if p is None:
                    pe.wait_ge(x1t_all_ok, NB)
                else:
                    wait(pe, place_ok, p)
                for c in range(2):
                    t = nc.tensor.transpose(bank[7][0:C, P * c:P * (c + 1)], ctx_in[:, slot, c, :], ident[:, :])
                t.then_inc(ctxt_ps, 1)

            def keys(n, q, i):
                if i == 0:
                    pe.wait_ge(ctxt_lo_ok, n + 1)
                wait(pe, kz_ok, 16 * n + i - 1)
                for c in range(2):
                    h = 2 * i + c
                    o = bank[4 + i % 2][:, 256 * c:256 * (c + 1)]
                    ah, al = a_hi[:, h % 2, h // 2, :], a_lo[:, h % 2, h // 2, :]
                    mm(o, ah, ctxt_hi[:, q, :], start=True, stop=False)
                    mm(o, ah, ctxt_lo[:, q, :], start=False, stop=False)
                    m = mm(o, al, ctxt_hi[:, q, :], start=False, stop=True)
                m.then_inc(kz_ps, 1)

            def values(n, q, i):
                pair, b, half = i // 4, i // 2 % 2, i % 2
                wait(pe, kz_ok, 16 * n + 8 + i - 1)
                at = P * pair + L * b
                for h2 in range(2):
                    m = mm(bank[4 + i % 2][DH * h2:DH * (h2 + 1), :], ctxt[:, q, at:at + L],
                           b_sb[:, h2, 4 * half:4 * half + 4, :].rearrange("c a d -> c (a d)"), start=True, stop=True)
                m.then_inc(kz_ps, 1)

            def cross_scores(p, s):
                q, j = s // 2 % 2, s % 2
                pe.wait_ge(x1t_ok, p + 1)
                wait(pe, sub_ok, p)
                pe.wait_ge(kz_ok, 8 * (p - j) + 8)
                for half in range(2):
                    for b in range(2):
                        at = P * j + L * b
                        m = mm(bank[half][L * b:L * (b + 1), :].rearrange("q (h k) -> q h k", k=L),
                               x1t[:, s % 2, L * b:L * (b + 1)], kp_all[:, q, 8 * half:8 * half + 8, at:at + L],
                               start=True, stop=True)
                m.then_inc(s_ready, 1)

            def prob_transposes(p):
                pe.wait_ge(pn_ok, p + 1)
                wait(pe, pt_ok, p)
                for c in range(HP):
                    t = nc.tensor.transpose(pt_ps[:, c, :], pn_sb[:, 2 * c:2 * c + 2, :].rearrange("p a k -> p (a k)"),
                                            ident[:, :])
                t.then_inc(pt_ready, 1)

            def attend(p, s):
                q, j = s // 2 % 2, s % 2
                pe.wait_ge(pt_ok, p + 1)
                wait(pe, r2_ok, p)
                pe.wait_ge(kz_ok, 8 * (p - j) + 16)
                for c in range(HP):
                    for b in range(2):
                        m = mm(bank[6][L * b:L * (b + 1), 0:D], pt_sb[:, c, L * b:L * (b + 1)],
                               z_all[:, q, j, b, c, :], start=(c == 0), stop=(c == HP - 1))
                m.then_inc(o2_ps, 1)

            def x2_transpose(p, j, has_ctx):
                pe.wait_ge(x2_ok, p + 1)
                wait(pe, place_ok, p)
                if has_ctx is not None:
                    pe.wait_ge(ctxt_ok, has_ctx + 1)
                nc.tensor.transpose(bank[7][:, 0:P], row[:, j, 0:D], ident[:, :]).then_inc(x2t_ps, 1)

            def router_logits(p):
                pe.wait_ge(x2t_ok, p + 1)
                mm(bank[7][:, 256:256 + E], x2t[:, :], wr_sb[:, :], start=True, stop=True).then_inc(lg_ps, 1)

            def ranks(p):
                pe.wait_ge(oh_ok, p + 1)
                wait(pe, seen_up, p)
                o = bank[7][:, 384:384 + E]
                mm(o, before_b[:, :], oh_b[:, :], start=True, stop=False)
                mm(o, ones_b[:, :], seen_b[:, :], start=False, stop=True).then_inc(rank_ps, 1)

            def slot(p, s, last=False):
                j = s % 2
                more = not (last and s >= 2)
                n, q = blk(p) + 1, (s // 2 + 1) % 2

                def kz(*groups):
                    if more:
                        for i in groups:
                            (keys, values)[j](n, q, i)

                prob_transposes(p)
                if not (last and s == 3):
                    cross_scores(p + 1, s + 1)
                if not (isinstance(p, int) and p == 0):
                    ranks(p - 1)
                kz(0, 1)
                attend(p, s)
                kz(2)
                has_ctx = j == 1 and not (last and s >= 1)
                if has_ctx:
                    ctx_transposes(n + 1, (s // 2) % 2, p)
                kz(3, 4, 5)
                x2_transpose(p, j, n + 1 if has_ctx else None)
                kz(6)
                router_logits(p)
                kz(7)

            def blk(p):
                return p // 2 if isinstance(p, int) else blk_of[0]

            blk_of = [None]

            pe.wait_ge(b1t_ok, 1)
            ctx_transposes(0, 0)
            ctx_transposes(1, 1)
            pe.wait_ge(b_ok, 4)
            pe.wait_ge(ssv_ok, NB)
            for i in range(8):
                keys(0, 0, i)
            for i in range(8):
                values(0, 0, i)
            cross_scores(0, 0)
            for s in range(4):
                slot(s, s)
            with pe.Fori(1, NT // 4 - 1) as i:
                for s in range(4):
                    blk_of[0] = 2 * i + s // 2
                    slot(4 * i + s, s)
            for s in range(4):
                slot(NT - 4 + s, s, last=True)
            ranks(NT - 1)
            pe.wait_ge(seen_up, NT)
            mm(bank[7][:, 384:384 + E], ones_b[:, :], seen_b[:, :], start=True, stop=True).then_inc(count_ps, 1)

            def transpose_rows(i, u):
                t = U * i + u
                pe.wait_ge(xs_ok[u], 16 * (i + 1))
                wait(pe, xst_ok, t - 1)
                nc.tensor.transpose(bank[u % 2][:, 0:P], xs[:, u, 0:D], ident[:, :]).then_inc(xst_ps, 1)

            def hidden(i, u):
                t = U * i + u
                pe.wait_ge(xst_ok, t + 1)
                pe.wait_ge(ew_ok, t + 1)
                wait(pe, h_ok, FC * (t - 1))
                for c in range(FC):
                    m = mm(bank[2 + u % 2][:, P * c:P * (c + 1)], ew[:, u, P * c:P * (c + 1)], xst[:, u % 2, :],
                           start=True, stop=True)
                m.then_inc(h_ps, 1)

            def project(i, u):
                t = U * i + u
                wait(pe, yb_ok, t - 1)
                e = pe.value_load(expert_of[0:1, bass.ds(t, 1)], min_val=0, max_val=E - 1)
                pe.wait_ge(h_ok, FC * (t + 1))
                for c in range(FC):
                    m = mm(bank[4 + u % 2][:, 0:D], ht[:, u % 2, c, :], w2_all[:, bass.ds(e, 1), c, :],
                           start=(c == 0), stop=(c == FC - 1))
                m.then_inc(y_ps, 1)

            def slot(i, u):
                if ahead(i, u, 2):
                    transpose_rows(*ahead(i, u, 2))
                if ahead(i, u, 1):
                    hidden(*ahead(i, u, 1))
                project(i, u)

            pe.wait_ge(table_ok, 1)
            pe.wait_ge(experts_in_ok, 48)
            transpose_rows(0, 0)
            transpose_rows(0, 1)
            hidden(0, 0)
            tiles(pe, slot)

        @block.scalar
        def _(act):
            a = nc.scalar.activation
            for n in range(NB):
                act.wait_ge(xt_ps, n + 1)
                wait(act, sc_ps, SC * n)
                a(x_hi[:, :], bank[1], ACT.Copy).then_inc(x_hi_ok, 1)
                wait(act, o1_ps, n - 1)
                for c in range(SC + 1):
                    if c < SC:
                        act.wait_ge(sc_ps, SC * n + c + 1)
                        a(g_sb[:, n % 2, c, :], bank[2 + c % 2], ACT.Gelu).then_inc(gelu_ok, 1)
                    if c >= 1:
                        act.wait_ge(gelu_ok, SC * n + c)
                        wait(act, sqsum_ok, 2 * n)
                        a(sq_sb[:, c - 1, :], g_sb[:, n % 2, c - 1, :], ACT.Square).then_inc(sq_ok, 1)
                if n >= 2:
                    act.wait_ge(x1t_ps, n - 1)
                    a(x1t_all[:, 512 * (n - 2):512 * (n - 1)], bank[7], ACT.Copy).then_inc(x1t_all_ok, 1)

            act.wait_ge(x1t_ps, NB - 1)
            a(x1t_all[:, 512 * (NB - 2):512 * (NB - 1)], bank[7], ACT.Copy).then_inc(x1t_all_ok, 1)
            for i in range(6):
                act.wait_ge(wt_ps, i + 1)
                dst, rows = ((wqt, P), (wkt, C), (wvt, C))[i // 2]
                a(dst[:, 4 * (i % 2):4 * (i % 2) + 4, :],
                  bank[i % 2].rearrange("p (c n) -> p c n", n=P)[:, :, 0:rows], ACT.Copy).then_inc(wt_ok, 1)
            for i in range(8):
                act.wait_ge(ab_ps, i + 1)
                half, h2 = i // 2 % 2, i % 2
                src = bank[2 + i % 4][0:C, :].rearrange("c (a d) -> c a d", d=D)
                if i < 4:
                    a(a_hi[:, h2, 4 * half:4 * half + 4, :], src, ACT.Copy).then_inc(a_hi_ok, 1)
                else:
                    a(b_sb[:, h2, 4 * half:4 * half + 4, :], src, ACT.Copy).then_inc(b_ok, 1)
            act.wait_ge(x1t_ps, NB)
            a(x1t_all[:, 512 * (NB - 1):512 * NB], bank[7], ACT.Copy).then_inc(x1t_all_ok, 1)
            act.wait_ge(b1t_ps, 1)
            a(ew_all[:, :, F:F + FC], bank[0][:, 0:E * FC].rearrange("p (e c) -> p e c", c=FC), ACT.Copy
              ).then_inc(b1t_ok, 1)

            def ctx_copy(n, slot):
                act.wait_ge(ctxt_ps, n + 1)
                a(ctxt[:, slot, :], bank[7][0:C, 0:256], ACT.Copy).then_inc(ctxt_ok, 1)

            def kz_copy(n, q, k):
                act.wait_ge(kz_ps, 16 * n + k + 1)
                src = bank[4 + k % 2]
                if k < 8:
                    dst = kp_all[:, q, 2 * k:2 * k + 2, :]
                    src = src.rearrange("p (c t) -> p c t", t=256)
                else:
                    i = k - 8
                    pair, b, half = i // 4, i // 2 % 2, i % 2
                    dst = z_all[:, q, pair, b, 4 * half:4 * half + 4, :]
                    src = src.rearrange("p (c t) -> p c t", t=D)
                a(dst, src, ACT.Copy).then_inc(kz_ok, 1)

            def exps(p):
                act.wait_ge(sub_ok, p + 1)
                wait(act, pn_ok, p)
                a(pe_sb[:, :, :], ps_sb[:, :, :], ACT.Exp, scale=SCALE).then_inc(exp_ok, 1)

            def gate_exp(p):
                act.wait_ge(ld_ok, p + 1)
                wait(act, row_ok, p)
                a(lexp[:, :], ld[:, :], ACT.Exp, accum_out=lsum[:, :]).then_inc(lsum_ok, 1)

            def prob_copy(p):
                act.wait_ge(pt_ready, p + 1)
                a(pt_sb[:, :, :], pt_ps, ACT.Copy).then_inc(pt_ok, 1)

            def x2t_copy(p):
                act.wait_ge(x2t_ps, p + 1)
                a(x2t[:, :], bank[7][:, 0:P], ACT.Copy).then_inc(x2t_ok, 1)

            def slot(p, s, n, last=False):
                j, q = s % 2, (s // 2 + 1) % 2

                def kz(*groups):
                    if not (last and s >= 2):
                        for k in groups:
                            kz_copy(n, q, 8 * j + k)

                prob_copy(p)
                kz(0)
                if not (isinstance(p, int) and p == 0):
                    gate_exp(p - 1)
                kz(1)
                if not (last and s == 3):
                    exps(p + 1)
                kz(2)
                if j == 1 and not (last and s >= 1):
                    ctx_copy(n + 1, (s // 2) % 2)
                kz(3, 4, 5)
                x2t_copy(p)
                kz(6, 7)

            ctx_copy(0, 0)
            ctx_copy(1, 1)
            for k in range(16):
                kz_copy(0, 0, k)
            exps(0)
            for s in range(4):
                slot(s, s, s // 2 + 1)
            with act.Fori(1, NT // 4 - 1) as i:
                for s in range(4):
                    slot(4 * i + s, s, 2 * i + s // 2 + 1)
            for s in range(4):
                slot(NT - 4 + s, s, (NT - 4 + s) // 2 + 1, last=True)
            gate_exp(NT - 1)

            def transposed_copy(i, u):
                t = U * i + u
                act.wait_ge(xst_ps, t + 1)
                wait(act, h_ps, t - 1)
                a(xst[:, u % 2, :], bank[u % 2][:, 0:P], ACT.Copy).then_inc(xst_ok, 1)

            def gelus(i, u):
                t = U * i + u
                act.wait_ge(h_ps, t + 1)
                wait(act, y_ps, t - 1)
                for c in range(FC):
                    a(ht[:, u % 2, c, :], bank[2 + u % 2][:, P * c:P * (c + 1)], ACT.Gelu,
                      bias=ew[:, u, F + c:F + c + 1]).then_inc(h_ok, 1)

            def slot(i, u):
                if ahead(i, u, 2):
                    transposed_copy(*ahead(i, u, 2))
                if ahead(i, u, 1):
                    gelus(*ahead(i, u, 1))

            transposed_copy(0, 0)
            transposed_copy(0, 1)
            gelus(0, 0)
            tiles(act, slot)

        @block.vector
        def _(dve):
            v = nc.vector
            dve.wait_ge(keyt_ps, 1)
            v.tensor_copy(key_hi[:, :], bank[0]).then_inc(key_hi_ok, 1)
            dve.wait_ge(key_hi_ok, 1)
            v.tensor_tensor(key_lo[:, :], bank[0], key_hi[:, :].bitcast(F32), ALU.subtract).then_inc(key_lo_ok, 1)

            def split_x(n):
                dve.wait_ge(x_hi_ok, n + 1)
                wait(dve, sc_ps, SC * n)
                v.tensor_tensor(x_lo[:, :], bank[1], x_hi[:, :].bitcast(F32), ALU.subtract).then_inc(x_lo_ok, 1)

            def norm1(n):
                dve.wait_ge(ss_ps, n + 1)
                wait(dve, inv_ok, n)
                v.tensor_scalar(ssv[:, :], bank[6][:, 0:4], 1.0 / S, None, ALU.mult).then_inc(ssv_ok, 1)
                dve.wait_ge(inv_ok, n + 1)
                dve.wait_ge(o1_ps, n + 1)
                wait(dve, x1_ok, n)
                for t in range(4):
                    m = v.scalar_tensor_tensor(r1[:, t, :], bank[4 + n % 2][:, P * t:P * (t + 1)], inv[:, t:t + 1],
                                               x_in[:, n, t, :], ALU.mult, ALU.add)
                m.then_inc(r1_ok, 1)
                dve.wait_ge(r1_ok, n + 1)
                for t in range(4):
                    m = v.bn_stats(st1[:, t, :], r1[:, t, :])
                m.then_inc(st1_ok, 1)
                dve.wait_ge(st1_ok, n + 1)
                wait(dve, ve1_ok, n)
                for t in range(4):
                    m = v.bn_aggr(mv1[:, t, :], st1[:, t, :])
                m.then_inc(mv1_ok, 1)
                dve.wait_ge(rs1_ok, n + 1)
                wait(dve, x1t_ps, n - 1)
                wait(dve, x1b_ok, n - 1)
                for t in range(4):
                    m = v.tensor_scalar(x1[:, n % 2, t, :], r1[:, t, :], mv1[:, t, 0:1], rs1[:, t:t + 1],
                                        ALU.subtract, ALU.mult)
                m.then_inc(x1_ok, 1)

            for n in range(NB):
                split_x(n)
                if n >= 1:
                    norm1(n - 1)
                wait(dve, ss_ps, n - 1)
                for c in range(2):
                    dve.wait_ge(sq_ok, SC * n + 2 * c + 2)
                    v.tensor_tensor(ss_sb[:, n % 2, c, :], sq_sb[:, 2 * c, :], sq_sb[:, 2 * c + 1, :], ALU.add
                                    ).then_inc(sqsum_ok, 1)
            norm1(NB - 1)
            for i in range(4):
                dve.wait_ge(a_hi_ok, i + 1)
                half, h2 = i // 2, i % 2
                v.tensor_tensor(a_lo[:, h2, 4 * half:4 * half + 4, :],
                                bank[2 + i][0:C, :].rearrange("c (a d) -> c a d", d=D),
                                a_hi[:, h2, 4 * half:4 * half + 4, :].bitcast(F32), ALU.subtract).then_inc(a_lo_ok, 1)

            def split_ctx(n, slot):
                dve.wait_ge(ctxt_ok, n + 1)
                wait(dve, kz_ps, 16 * (n - 1) - 8)
                v.tensor_copy(ctxt_hi[:, slot, :], ctxt[:, slot, :]).then_inc(ctxt_hi_ok, 1)
                dve.wait_ge(ctxt_hi_ok, n + 1)
                v.tensor_tensor(ctxt_lo[:, slot, :], ctxt[:, slot, :], ctxt_hi[:, slot, :].bitcast(F32), ALU.subtract
                                ).then_inc(ctxt_lo_ok, 1)

            def heads(t):
                return t[:, :].unsqueeze(2).broadcast_to([P, H, L])

            def maxes(p):
                dve.wait_ge(s_ready, p + 1)
                v.reduce_max(smax[:, :], s_ps, AX.X).then_inc(max_ok, 1)

            def subtract_max(p):
                dve.wait_ge(max_ok, p + 1)
                wait(dve, exp_ok, p)
                v.tensor_tensor(ps_sb[:, :, :], s_ps, heads(smax), ALU.subtract).then_inc(sub_ok, 1)

            def sums(p):
                dve.wait_ge(exp_ok, p + 1)
                v.reduce_sum(psum_l[:, :], pe_sb[:, :, :], AX.X).then_inc(sum_ok, 1)

            def normalise(p):
                dve.wait_ge(sum_ok, p + 1)
                v.reciprocal(pinv[:, :], psum_l[:, :]).then_inc(pinv_ok, 1)
                dve.wait_ge(pinv_ok, p + 1)
                wait(dve, pt_ready, p)
                v.tensor_tensor(pn_sb[:, :, :], pe_sb[:, :, :], heads(pinv), ALU.mult).then_inc(pn_ok, 1)

            def at(tensor, p):
                return tensor[:, p, :] if isinstance(p, int) else tensor[:, bass.ds(p, 1), :]

            def stats2(p):
                dve.wait_ge(o2_ps, p + 1)
                v.tensor_tensor(r2[:, :], bank[6][:, 0:D], at(x1b_all, p), ALU.add).then_inc(r2_ok, 1)
                dve.wait_ge(r2_ok, p + 1)
                v.bn_stats(st2[:, :], r2[:, :]).then_inc(st2_ok, 1)
                waits_apart(dve, (x2_ok, p), (st2_ok, p + 1))
                v.bn_aggr(mv2[:, :], st2[:, :]).then_inc(mv2_ok, 1)

            def norm2(p, s):
                dve.wait_ge(rs2_ok, p + 1)
                if not (isinstance(p, int) and p < 2):
                    dve.wait_ge(scat_ok[s % 2], 8 * (p - s % 2))
                v.tensor_scalar(row[:, s % 2, 0:D], r2[:, :], mv2[:, 0:1], rs2[:, :], ALU.subtract, ALU.mult
                                ).then_inc(x2_ok, 1)

            def choose(p):
                dve.wait_ge(lg_ps, p + 1)
                v.tensor_tensor(lg[:, :], bank[7][:, 256:256 + E], br_all[:, :], ALU.add).then_inc(lg_ok, 1)
                waits_apart(dve, (lg_ok, p + 1))
                v.max(lmax[:, :], lg[:, :]).then_inc(lmax_ok, 1)
                waits_apart(dve, (lmax_ok, p + 1))
                v.max_index(lidx[:, :], lmax[:, :], lg[:, :]).then_inc(lidx_ok, 1)
                v.tensor_scalar(ld[:, :], lg[:, :], lmax[:, 0:1], None, ALU.subtract).then_inc(ld_ok, 1)
                dve.wait_ge(lidx_ok, p + 1)
                v.tensor_copy(lidf[:, :], lidx[:, 0:1]).then_inc(lidf_ok, 1)
                dve.wait_ge(lidf_ok, p + 1)
                wait(dve, rank_ps, p)
                v.tensor_scalar(oh_b[:, :], expert_no[:, :], lidf[:, :], None, ALU.is_equal).then_inc(oh_ok, 1)

            def finish_row(p, s):
                dve.wait_ge(rank_ps, p + 1)
                v.tensor_tensor(place[:, :], bank[7][:, 384:384 + E], region_base[:, :], ALU.add
                                ).then_inc(place_ok, 1)
                v.tensor_tensor(seen_b[:, :], seen_b[:, :], oh_b[:, :], ALU.add).then_inc(seen_up, 1)
                dve.wait_ge(place_ok, p + 1)
                v.tensor_tensor(placed[:, :], place[:, :], oh_b[:, :], ALU.mult).then_inc(placed_ok, 1)
                dve.wait_ge(lsum_ok, p + 1)
                v.reciprocal(row[:, s % 2, GATE:GATE + 1], lsum[:, :])
                src = token_no[:, p:p + 1] if isinstance(p, int) else token_no[:, bass.ds(p, 1)]
                v.tensor_copy(row[:, s % 2, TOKEN:TOKEN + 1].bitcast(I32), src).then_inc(row_ok, 1)
                dve.wait_ge(placed_ok, p + 1)
                v.reduce_sum(posf[:, :], placed[:, :], AX.X).then_inc(placed2, 1)
                dve.wait_ge(placed2, p + 1)
                v.tensor_copy(posi[:, s % 2:s % 2 + 1], posf[:, :]).then_inc(pos_ok, 1)

            def slot(p, s, n, last=False):
                more = not (last and s == 3)
                if more:
                    maxes(p + 1)
                    subtract_max(p + 1)
                if not (isinstance(p, int) and p == 0):
                    finish_row(p - 1, (s - 1) % 2)
                stats2(p)
                if more:
                    sums(p + 1)
                norm2(p, s)
                if more:
                    normalise(p + 1)
                if s % 2 == 1 and not (last and s >= 1):
                    split_ctx(n + 1, (s // 2) % 2)
                choose(p)

            split_ctx(0, 0)
            split_ctx(1, 1)
            maxes(0)
            subtract_max(0)
            sums(0)
            normalise(0)
            for s in range(4):
                slot(s, s, s // 2 + 1)
            with dve.Fori(1, NT // 4 - 1) as i:
                for s in range(4):
                    slot(4 * i + s, s, 2 * i + s // 2 + 1)
            for s in range(4):
                slot(NT - 4 + s, s, (NT - 4 + s) // 2 + 1, last=True)
            finish_row(NT - 1, 1)

            steps = [0]

            def step(ins):
                steps[0] += 1
                ins.then_inc(tab, 1)
                dve.wait_ge(tab, steps[0])

            dve.wait_ge(count_ps, 1)
            dve.wait_ge(seen_ok, 6)
            counts = bank[7][0:1, 384:384 + E]
            step(v.tensor_tensor(pad_at[:, :], counts, region_base[0:1, :], ALU.add))
            step(v.tensor_scalar(n_int[:, :], counts, float(P - 1), None, ALU.add))
            step(v.tensor_scalar(n_sh[:, :], n_int[:, :], 7, None, ALU.logical_shift_right))
            step(v.tensor_copy(tiles_e[:, :], n_sh[:, :]))
            step(v.tensor_scalar(tl_skip[:, :], tiles_e[:, :], -float(P), float(REGION), ALU.mult, ALU.add))
            step(v.tensor_tensor(tl_mul[:, :, :], tiles_e[:, :].unsqueeze(1).broadcast_to([1, E, E]),
                                 le_expert[:, :, :], ALU.mult))
            step(v.reduce_sum(tl_end[:, :], tl_mul[:, :, :], AX.X))
            wide = [1, TILES, E]
            step(v.tensor_tensor(past[:, :, :], tl_end[:, :].unsqueeze(1).broadcast_to(wide), tile_no[:, :, :],
                                 ALU.is_le))
            step(v.reduce_sum(past_n[:, :], past[:, :, :], AX.X))
            step(v.tensor_scalar(expert_of[:, :], past_n[:, :], float(E - 1), None, ALU.min))
            step(v.tensor_tensor(skip[:, :, :], past[:, :, :], tl_skip[:, :].unsqueeze(1).broadcast_to(wide),
                                 ALU.mult))
            step(v.reduce_sum(skip_n[:, :], skip[:, :, :], AX.X))
            v.tensor_tensor(row_of[:, :], skip_n[:, :], tile_row[:, :], ALU.add).then_inc(table_ok, 1)
            dve.wait_ge(table_ok, 1)
            dve.wait_ge(experts_in_ok, 48)
            dve.wait_ge(b1t_ok, 1)

            def expert_copy(i, u):
                t = U * i + u
                e = dve.value_load(expert_of[0:1, bass.ds(t, 1)], min_val=0, max_val=E - 1)
                wait(dve, h_ok, FC * (t - U + 1))
                v.tensor_copy(ew[:, u, :], ew_all[:, bass.ds(e, 1), :]).then_inc(ew_ok, 1)

            def norm3(i, u):
                t = U * i + u
                dve.wait_ge(rs3_ok, t + 1)
                if not (isinstance(i, int) and i == 0):
                    dve.wait_ge(out_ok[u], 16 * i)
                v.tensor_scalar(ot[:, u, :], r3[:, u % 2, :], mv3[:, u % 2, 0:1], rs3[:, u % 2, :],
                                ALU.subtract, ALU.mult).then_inc(o3_ok, 1)

            def slot(i, u):
                t, b = U * i + u, u % 2
                dve.wait_ge(y_ps, t + 1)
                dve.wait_ge(ew_ok, t + 1)
                v.tensor_tensor(yb[:, b, :], bank[4 + b][:, 0:D], ew[:, u, F + FC:EW], ALU.add).then_inc(yb_ok, 1)
                if ahead(i, u, 3):
                    expert_copy(*ahead(i, u, 3))
                dve.wait_ge(yb_ok, t + 1)
                dve.wait_ge(xs_ok[u], 16 * (i + 1))
                v.scalar_tensor_tensor(r3[:, b, :], yb[:, b, :], xs[:, u, GATE:GATE + 1], xs[:, u, 0:D],
                                       ALU.mult, ALU.add).then_inc(r3_ok, 1)
                if not (isinstance(i, int) and t == 0):
                    norm3(*((i, u - 1) if u else (i - 1, U - 1)))
                dve.wait_ge(r3_ok, t + 1)
                v.bn_stats(st3[:, b, :], r3[:, b, :]).then_inc(st3_ok, 1)
                waits_apart(dve, (st3_ok, t + 1))
                v.bn_aggr(mv3[:, b, :], st3[:, b, :]).then_inc(mv3_ok, 1)

            for u in range(3):
                expert_copy(0, u)
            tiles(dve, slot)
            norm3(ROUNDS - 1, U - 1)


_INS = ["x", "ctx_768", "L0_attn_key_param_tokens", "L0_attn_value_param_tokens", "L0_xattn_Wq", "L0_xattn_Wk",
        "L0_xattn_Wv", "L0_xattn_Wo", "L0_xattn_bo", "L0_ffn_W1", "L0_ffn_b1", "L0_ffn_W2", "L0_ffn_b2",
        "L0_ffn_Wr", "L0_ffn_br"]


def kernel(**inputs):
    import numpy as np
    import concourse.bacc as bacc
    from concourse import mybir as mb
    from concourse.bass_utils import run_bass_kernel_spmd

    nc = bacc.Bacc("TRN2", target_bir_lowering=False, num_devices=1)
    arrays, args = {}, []
    for name in _INS:
        a = np.ascontiguousarray(inputs[name])
        arrays[f"in_{name}"] = a
        args.append(nc.dram_tensor(f"in_{name}", a.shape, mb.dt.from_np(a.dtype), kind="ExternalInput").ap())
    args.append(nc.dram_tensor("out", (32, 64, 128), mb.dt.float32, kind="ExternalOutput").ap())
    build_program(nc, *args)
    r = run_bass_kernel_spmd(nc, [arrays], core_ids=[0])
    return r.results[0]["out"]
```

```python
import math
from contextlib import ExitStack

import concourse.bass as bass
from concourse import mybir

ALU = mybir.AluOpType
ACT = mybir.ActivationFunctionType
F32 = mybir.dt.float32
F32R = mybir.dt.float32r
BF16 = mybir.dt.bfloat16
I32 = mybir.dt.int32
U32 = mybir.dt.uint32
AX = mybir.AxisListType

P = 128
EPS = 1e-5


def build_program(nc, x, ctx, key, value, wq, wk, wv, wo, bo, w1, b1, w2, b2, wr, br, out):
    B, L, D = x.shape
    C = ctx.shape[2]
    S = key.shape[0]
    INNER = wq.shape[1]
    DH = 64
    H = INNER // DH
    HP = H // 2
    E, _, F = w1.shape
    T = B * L
    NT = T // P
    SC = S // P
    FC = F // P
    NB = T // 512
    CB = T // 256
    assert D == P and L == DH and H * DH == INNER and T % 512 == 0
    U = 6
    TILES = NT + E - 1
    ROUNDS = -(-TILES // U)
    LAST = TILES - U * (ROUNDS - 1)
    REGION = T + P
    SPARE = TILES - NT
    PADDED = NT - 3
    PADS = NT - PADDED + 1
    ROW = D + 4
    GATE, TOKEN = D, D + 1
    EW = F + FC + D
    SCALE = 1.0 / 8.0

    xf = x.rearrange("b s d -> (b s) d")
    cf = ctx.rearrange("b s c -> (b s) c")
    of = out.rearrange("b s d -> (b s) d")
    routed = nc.dram_tensor("routed_rows", [E * REGION + SPARE * P, ROW], F32).ap()

    es = ExitStack()
    with es:
        def sb(name, shape, dt=F32):
            return es.enter_context(nc.sbuf_tensor(name, shape, dt))

        def pb(name, shape):
            return es.enter_context(nc.psum_tensor(name, shape, F32))

        def sem(name):
            return es.enter_context(nc.semaphore(name))

        ident = sb("ident", [P, P])
        ones = sb("ones", [P, 1])
        ones_b = sb("ones_b", [P, P], BF16)
        before_b = sb("before_b", [P, P], BF16)
        minus_half = sb("minus_half", [P, 4])
        eps = sb("eps", [P, 4])
        table_in = sb("table_in", [P, 1])
        expert_no = sb("expert_no", [P, E])
        region_base = sb("region_base", [P, E])
        token_no = sb("token_no", [P, NT], I32)
        tile_no = sb("tile_no", [1, TILES, E])
        tile_row = sb("tile_row", [1, TILES])
        le_expert = sb("le_expert", [1, E, E])
        pad_row = sb("pad_row", [P, PADS, ROW])
        bo_all = sb("bo_all", [P, D])
        br_all = sb("br_all", [P, E])
        wr_sb = sb("wr_sb", [P, E])
        key_in = sb("key_in", [P, SC, D])
        value_in = sb("value_in", [P, SC, D])
        split = sb("split", [P, 4, 512], F32R)
        key_hi, key_lo, x_hi, x_lo = (split[:, n, :] for n in range(4))
        b_lo = split[:, :, :].rearrange("p n k -> p (n k)")[0:C, :].rearrange("p (a c d) -> p a c d", a=2, c=HP)
        a_hi = sb("a_hi", [C, 2, HP, D], F32R)
        a_lo = sb("a_lo", [C, 2, HP, D], F32R)
        b_hi = sb("b_hi", [C, 2, HP, D], F32R)
        ew_all = sb("ew_all", [P, E, EW])
        w2_all = sb("w2_all", [P, E, FC, D])
        b1_in = sb("b1_in", [E * FC, P])
        x1b_all = sb("x1b_all", [P, NT, D])
        x1t_all = sb("x1t_all", [P, T])

        z_all = sb("z_all", [P, 2, 2, 2, HP, D])
        zf = z_all[:, :, :, :, :, :].rearrange("p a b c e d -> p (a b c e d)")
        wq_in = zf[:, 0:1024]
        wk_in = zf[0:C, 1024:2048]
        wv_in = zf[0:C, 2048:3072]
        wo_in = zf[:, 3072:4096].rearrange("p (c n) -> p c n", n=D)
        wqt = zf[:, 4096:5120].rearrange("p (c n) -> p c n", n=D)
        wkt = zf[:, 5120:5888].rearrange("p (c n) -> p c n", n=C)
        wvt = zf[:, 5888:6656].rearrange("p (c n) -> p c n", n=C)

        kp_all = sb("kp_all", [P, 2, H, 256])
        kf = kp_all[:, :, :, :].rearrange("p a h t -> p (a h t)")
        g_sb = kf[:, 0:4096].rearrange("p (a c t) -> p a c t", a=2, c=SC)
        sq_sb = kf[:, 4096:6144].rearrange("p (c t) -> p c t", c=SC)
        sq2 = kf[:, 6144:7168].rearrange("p (c t) -> p c t", c=2)
        ss_sb = kf[:, 7168:8192].rearrange("p (a t) -> p a t", a=2)

        x_in = sb("x_in", [P, NB, 4, D])
        ssv = sb("ssv", [P, 4])
        inv = sb("inv", [P, 4])
        r1 = sb("r1", [P, 4, D])
        st1 = sb("st1", [P, 4, 6])
        mv1 = sb("mv1", [P, 4, 2])
        ve1 = sb("ve1", [P, 4])
        rs1 = sb("rs1", [P, 4])
        x1 = sb("x1", [P, 2, 4, D])

        ctx_in = sb("ctx_in", [P, 2, 2, C])
        ctxt = sb("ctxt", [C, 2, 256])
        ctxt_hi = sb("ctxt_hi", [C, 2, 256], F32R)
        ctxt_lo = sb("ctxt_lo", [C, 2, 256], F32R)
        x1t = sb("x1t", [P, 2, P])
        smax = sb("smax", [P, H])
        ps_sb = sb("ps_sb", [P, H, L])
        pe_sb = sb("pe_sb", [P, H, L])
        prob_sum = sb("prob_sum", [P, H])
        pinv = sb("pinv", [P, H])
        pn_sb = sb("pn_sb", [P, H, L])
        pt_sb = sb("pt_sb", [P, HP, P])
        r2 = sb("r2", [P, D])
        st2 = sb("st2", [P, 6])
        mv2 = sb("mv2", [P, 2])
        ve2 = sb("ve2", [P, 1])
        rs2 = sb("rs2", [P, 1])
        row = sb("row", [P, 2, ROW])
        x2t = sb("x2t", [P, P])
        lg = sb("lg", [P, E])
        lmax = sb("lmax", [P, 8])
        lidx = sb("lidx", [P, 8], U32)
        lidf = sb("lidf", [P, 1])
        ld = sb("ld", [P, E])
        lexp = sb("lexp", [P, E])
        lsum = sb("lsum", [P, 1])
        oh_b = sb("oh_b", [P, E], BF16)
        seen_b = sb("seen_b", [P, E], BF16)
        place = sb("place", [P, E])
        placed = sb("placed", [P, E])
        posf = sb("posf", [P, 1])
        posi = sb("posi", [P, 2], I32)

        n_int = sb("n_int", [1, E], I32)
        n_tiles = sb("n_tiles", [1, E], I32)
        tl_mul = sb("tl_mul", [1, E, E])
        tl_end = sb("tl_end", [1, E])
        tl_skip = sb("tl_skip", [1, E])
        past = sb("past", [1, TILES, E])
        past_n = sb("past_n", [1, TILES])
        skip = sb("skip", [1, TILES, E])
        skip_n = sb("skip_n", [1, TILES])
        expert_of = sb("expert_of", [1, TILES], I32)
        row_of = sb("row_of", [1, TILES], I32)
        pad_at = sb("pad_at", [1, E], I32)

        taken = [0]

        def part(*shape):
            size = math.prod(shape)
            at, taken[0] = taken[0], taken[0] + size
            assert taken[0] <= 2 * H * 256
            flat = kf[:, at:at + size]
            if len(shape) == 1:
                return flat
            if len(shape) == 2:
                return flat.rearrange("p (a n) -> p a n", n=shape[1])
            return flat.rearrange("p (a c n) -> p a c n", c=shape[1], n=shape[2])

        xs = part(U, ROW)
        token = part(U, 1)
        ew = part(U, EW)
        xst = part(2, P)
        ht = part(2, FC, P)
        yb = part(2, D)
        r3 = part(3, D)
        st3 = part(3, 6)
        mv3 = part(3, 2)
        rs3 = part(3, 1)
        ve3 = part(3, 1)
        ot = part(U, D)

        b01 = pb("b01", [P, 1024])
        b23 = pb("b23", [P, 1024])
        b4 = pb("b4", [P, 512])
        b5 = pb("b5", [P, 512])
        b6 = pb("b6", [P, 512])
        b7 = pb("b7", [P, 512])
        bank = [b01[:, 0:512], b01[:, 512:1024], b23[:, 0:512], b23[:, 512:1024],
                b4[:, :], b5[:, :], b6[:, :], b7[:, :]]
        o2_lasts = (bank[5][:, 256:384], bank[2][:, 256:384])
        o2_bank, lg_bank, rank_bank = bank[7][:, 256:384], bank[7][:, 384:392], bank[7][:, 400:408]

        def o2_of(p):
            return o2_lasts[p - NT] if isinstance(p, int) and p >= NT - 2 else o2_bank

        ring = bank[2:7]
        a_bank, b_bank = bank[2:6], (bank[0], bank[1], bank[6], bank[5])
        sc_bank = (bank[2], bank[3], bank[0])
        s_ps = b01[:, :].rearrange("p (h k) -> p h k", k=L)

        key_in_ok, value_in_ok, ctx_in_ok = sem("key_in_ok"), sem("value_in_ok"), [sem("ctx_in_ok0"), sem("ctx_in_ok1")]
        x_in_ok = [sem(f"x_in_ok{n}") for n in range(NB)]
        wqk_in_ok, wvo_in_ok, small_in_ok = sem("wqk_in_ok"), sem("wvo_in_ok"), sem("small_in_ok")
        experts_in_ok = sem("experts_in_ok")
        const_ok, seen_ok = sem("const_ok"), sem("seen_ok")
        keyt_ps, key_hi_ok, key_lo_ok = sem("keyt_ps"), sem("key_hi_ok"), sem("key_lo_ok")
        xt_ps, x_hi_ok, x_lo_ok = sem("xt_ps"), sem("x_hi_ok"), sem("x_lo_ok")
        sc_ps, gelu_ok, sq_ok = sem("sc_ps"), sem("gelu_ok"), sem("sq_ok")
        sqsum_ok, o1_ps, ss_ps = sem("sqsum_ok"), sem("o1_ps"), sem("ss_ps")
        ssv_ok, inv_ok = sem("ssv_ok"), sem("inv_ok")
        r1_ok, st1_ok, mv1_ok, ve1_ok, rs1_ok = sem("r1_ok"), sem("st1_ok"), sem("mv1_ok"), sem("ve1_ok"), sem("rs1_ok")
        x1_ok, x1b_ok, x1t_ps, x1t_all_ok = sem("x1_ok"), sem("x1b_ok"), sem("x1t_ps"), sem("x1t_all_ok")
        wt_ps, wt_ok, ab_ps, a_hi_ok, a_lo_ok, b_ok = (sem("wt_ps"), sem("wt_ok"), sem("ab_ps"), sem("a_hi_ok"),
                                                         sem("a_lo_ok"), sem("b_ok"))
        b_lo_ok = sem("b_lo_ok")
        b1t_ps, b1t_ok = sem("b1t_ps"), sem("b1t_ok")
        ctxt_ps, ctxt_ok, ctxt_hi_ok, ctxt_lo_ok = sem("ctxt_ps"), sem("ctxt_ok"), sem("ctxt_hi_ok"), sem("ctxt_lo_ok")
        kz_ps, kz_ok, z_ok = sem("kz_ps"), sem("kz_ok"), sem("z_ok")
        x1t_ok, s_ready, max_ok, sub_ok, exp_ok, sum_ok, pinv_ok, pn_ok = (
            sem("x1t_ok"), sem("s_ready"), sem("max_ok"), sem("sub_ok"), sem("exp_ok"), sem("sum_ok"),
            sem("pinv_ok"), sem("pn_ok"))
        pt_ready, pt_ok, o2_ps = sem("pt_ready"), sem("pt_ok"), sem("o2_ps")
        r2_ok, st2_ok, mv2_ok, ve2_ok, rs2_ok, x2_ok = (sem("r2_ok"), sem("st2_ok"), sem("mv2_ok"), sem("ve2_ok"),
                                                          sem("rs2_ok"), sem("x2_ok"))
        x2t_ps, x2t_ok, lg_ps, lg_ok, lmax_ok, lidx_ok, lidf_ok, oh_ok, ld_ok, lsum_ok = (
            sem("x2t_ps"), sem("x2t_ok"), sem("lg_ps"), sem("lg_ok"), sem("lmax_ok"), sem("lidx_ok"),
            sem("lidf_ok"), sem("oh_ok"), sem("ld_ok"), sem("lsum_ok"))
        rank_ps, place_ok, seen_up, placed_ok, placed2, row_ok, pos_ok = (
            sem("rank_ps"), sem("place_ok"), sem("seen_up"), sem("placed_ok"), sem("placed2"), sem("row_ok"),
            sem("pos_ok"))
        scat_ok = [sem("scat_ok0"), sem("scat_ok1")]
        count_ps, tab, table_ok = sem("count_ps"), sem("tab"), sem("table_ok")
        pad_at_ok, pad_ok, spare_ok = sem("pad_at_ok"), sem("pad_ok"), sem("spare_ok")
        xs_ok = [sem(f"xs_ok{n}") for n in range(U)]
        xst_ps, xst_ok, ew_ok, h_ps, h_ok, y_ps = (sem("xst_ps"), sem("xst_ok"), sem("ew_ok"), sem("h_ps"),
                                                     sem("h_ok"), sem("y_ps"))
        yb_ok, r3_ok, st3_ok, mv3_ok, ve3_ok, rs3_ok, o3_ok = (sem("yb_ok"), sem("r3_ok"), sem("st3_ok"),
                                                                 sem("mv3_ok"), sem("ve3_ok"), sem("rs3_ok"),
                                                                 sem("o3_ok"))
        token_ok = sem("token_ok")
        out_ok = [sem(f"out_ok{n}") for n in range(U)]

        CONSTS = 12

        def wait(eng, s, n):
            if not isinstance(n, int) or n > 0:
                eng.wait_ge(s, n)

        def waits_apart(eng, *waits):
            counts = [n if isinstance(n, int) else eng.to_reg(n) for _, n in waits]
            eng.wait_ge(const_ok, 1)
            for (s, _), n in zip(waits, counts):
                wait(eng, s, n)

        def tiles(eng, slot):
            for u in range(U):
                slot(0, u)
            with eng.Fori(1, ROUNDS - 1) as i:
                for u in range(U):
                    slot(i, u)
            for u in range(LAST):
                slot(ROUNDS - 1, u)

        KEYS, VALUES = "keys", "values"
        opening = ([(0, KEYS, i) for i in range(8)] + [(0, VALUES, 0), (0, VALUES, 1)] +
                   [(1, KEYS, 0), (0, VALUES, 2), (1, KEYS, 1), (0, VALUES, 3), (0, VALUES, 4)] +
                   [(1, KEYS, 2), (0, VALUES, 5), (1, KEYS, 3), (0, VALUES, 6), (0, VALUES, 7)])
        OPEN = len(opening)
        even = [(1, KEYS, 4), (1, VALUES, 0), (1, KEYS, 5), (1, KEYS, 6), (1, KEYS, 7), (1, VALUES, 2),
                (1, VALUES, 1), (1, VALUES, 3)]
        odd = [g for i in range(4) for g in ((1, VALUES, 4 + i), (2, KEYS, i))]

        def shared(g):
            return g[1] == VALUES and g[2] % 2 == 0

        SHARED = sum(map(shared, opening))

        def kz_of(at):
            return ring[(at if at == 0 else at + 2) % 5]

        HALVES = (ring[1], ring[2])

        GROUP_BEFORE = (-5, -2, -1, 0, None, None, 1, 2)
        HALF_BEFORE = (-4, -3)

        def places(s, last):
            if not last or s == 0:
                return list(enumerate((even, odd)[s % 2]))
            return list(enumerate((1, VALUES, g) for g in (4, 6, 5, 7))) if s == 1 else []

        GROUPS = 16 * CB

        def z_copy(copy, bank, q, g, b, h2, *how):
            pair, four = g[2] // 4, g[2] % 4
            src = bank[L * b:L * (b + 1), 256 * h2:256 * (h2 + 1)].rearrange("p (c d) -> p c d", d=D)
            return copy(z_all[L * h2:L * (h2 + 1), q, pair, b, 2 * four:2 * four + 2, :], src, *how)

        def ahead(i, u, n):
            if isinstance(i, int) and U * i + u + n >= TILES:
                return None
            return i + (u + n) // U, (u + n) % U

        def back(i, u, n):
            return (i, u - n) if u >= n else (i - 1, u - n + U)

        block = es.enter_context(nc.Block())

        @block.sync
        def _(sp):
            sp.dma_start(key_in[:, :, :], key.rearrange("(c p) d -> p c d", p=P)).then_inc(key_in_ok, 16)
            for n in range(NB):
                sp.dma_start(x_in[:, n, :, :], xf[512 * n:512 * (n + 1), :].rearrange("(c p) d -> p c d", p=P)
                             ).then_inc(x_in_ok[n], 16)
                if n == 0:
                    sp.dma_start(value_in[:, :, :], value.rearrange("(c p) d -> p c d", p=P)).then_inc(value_in_ok, 16)
            sp.dma_start(bo_all[:, :], bo.partition_broadcast(P)).then_inc(small_in_ok, 16)
            sp.dma_start(br_all[:, :], br.partition_broadcast(P)).then_inc(small_in_ok, 16)
            sp.dma_start(wr_sb[:, :], wr).then_inc(small_in_ok, 16)
            sp.dma_start(b1_in[:, :], b1.rearrange("e (c p) -> (e c) p", p=P)).then_inc(small_in_ok, 16)
            sp.dma_start(wq_in, wq).then_inc(wqk_in_ok, 16)
            sp.dma_start(wk_in, wk).then_inc(wqk_in_ok, 16)
            sp.dma_start(wv_in, wv).then_inc(wvo_in_ok, 16)
            sp.dma_start(wo_in, wo.rearrange("(c p) n -> p c n", p=P)).then_inc(wvo_in_ok, 16)
            for n in range(2):
                sp.dma_start(ctx_in[:, n, :, :], cf[256 * n:256 * (n + 1), :].rearrange("(c p) d -> p c d", p=P)
                             ).then_inc(ctx_in_ok[n], 16)
            sp.dma_start(ew_all[:, :, 0:F], w1.rearrange("e d f -> d e f")).then_inc(experts_in_ok, 16)
            sp.dma_start(ew_all[:, :, F + FC:EW], b2.partition_broadcast(P)).then_inc(experts_in_ok, 16)
            sp.dma_start(w2_all[:, :, :, :], w2.rearrange("e (c p) d -> p e c d", p=P)).then_inc(experts_in_ok, 16)
            sp.wait_ge(const_ok, CONSTS)
            for n in range(SPARE):
                sp.dma_start(routed[E * REGION + P * n:E * REGION + P * (n + 1), :], pad_row[:, 0, :]
                             ).then_inc(spare_ok, 16)

            def ctx_load(n, slot):
                sp.wait_ge(ctxt_ps, n - 1)
                sp.dma_start(ctx_in[:, slot, :, :],
                             cf[bass.ds(n * 256, 256), :].rearrange("(c p) d -> p c d", p=P)
                             ).then_inc(ctx_in_ok[slot], 16)

            with sp.Fori(0, (CB - 2) // 2) as i:
                ctx_load(2 * i + 2, 0)
                ctx_load(2 * i + 3, 1)

            sp.wait_ge(pad_at_ok, 1)
            for e in range(E):
                at = sp.value_load(pad_at[0:1, e:e + 1], min_val=e * REGION, max_val=e * REGION + T + P - PADS * P)
                sp.dma_start(routed[bass.ds(at, PADS * P), :].rearrange("(c p) r -> p c r", p=P), pad_row[:, :, :]
                             ).then_inc(pad_ok, 16)
            sp.wait_ge(table_ok, 1)
            sp.wait_ge(spare_ok, 16 * SPARE)
            for n in range(2):
                sp.wait_ge(scat_ok[n], 16 * (NT // 2))

            def tile_load(i, u):
                wait(sp, token_ok, U * i + u - U + 1)
                at = sp.value_load(row_of[0:1, bass.ds(U * i + u, 1)], min_val=0,
                                   max_val=E * REGION + (SPARE - 1) * P)
                sp.dma_start(xs[:, u, :], routed[bass.ds(at, P), :]).then_inc(xs_ok[u], 16)

            tiles(sp, tile_load)
            for u in range(U):
                sp.wait_ge(out_ok[u], 16 * (ROUNDS if u < LAST else ROUNDS - 1))

        @block.gpsimd
        def _(pl):
            g = nc.gpsimd
            g.memset(ident[:, :], 0.0).then_inc(const_ok, 1)
            pl.wait_ge(const_ok, 1)
            g.affine_select(out=ident[:, :], in_=ident[:, :], compare_op=ALU.not_equal, fill=1.0, base=0,
                            pattern=[[-1, P]], channel_multiplier=1).then_inc(const_ok, 1)
            g.memset(ones[:, :], 1.0).then_inc(const_ok, 1)
            g.memset(minus_half[:, :], -0.5).then_inc(const_ok, 1)
            g.memset(ones_b[:, :], 1.0).then_inc(const_ok, 1)
            g.memset(pad_row[:, :, :], 0.0).then_inc(const_ok, 1)
            pl.wait_ge(const_ok, 6)
            g.affine_select(out=before_b[:, :], in_=ones_b[:, :], compare_op=ALU.is_gt, fill=0.0, base=0,
                            pattern=[[1, P]], channel_multiplier=-1).then_inc(const_ok, 1)
            g.iota(pad_row[:, :, TOKEN].bitcast(I32), [[0, PADS]], base=2 * T, channel_multiplier=0
                   ).then_inc(const_ok, 1)
            g.iota(token_no[:, :], [[P, NT]], base=0, channel_multiplier=1).then_inc(const_ok, 1)
            g.iota(expert_no[:, :], [[1, E]], base=0, channel_multiplier=0,
                   allow_small_or_imprecise_dtypes=True).then_inc(const_ok, 1)
            g.iota(region_base[:, :], [[REGION, E]], base=0, channel_multiplier=0,
                   allow_small_or_imprecise_dtypes=True).then_inc(const_ok, 1)
            g.memset(row[:, :, TOKEN + 1:ROW], 0.0).then_inc(const_ok, 1)
            g.iota(tile_no[:, :, :], [[1, TILES], [0, E]], base=0, channel_multiplier=0,
                   allow_small_or_imprecise_dtypes=True).then_inc(seen_ok, 1)
            g.iota(tile_row[:, :], [[P, TILES]], base=0, channel_multiplier=0,
                   allow_small_or_imprecise_dtypes=True).then_inc(seen_ok, 1)
            g.memset(le_expert[:, :, :], 1.0).then_inc(seen_ok, 1)
            g.memset(seen_b[:, :], 0.0).then_inc(seen_ok, 1)
            g.memset(eps[:, :], EPS).then_inc(seen_ok, 1)
            pl.wait_ge(seen_ok, 5)
            last_routed, last_token = pl.to_reg(E * REGION - 1), pl.to_reg(T - 1)
            g.affine_select(out=le_expert[:, :, :], in_=le_expert[:, :, :], compare_op=ALU.is_ge, fill=0.0, base=0,
                            pattern=[[1, E], [-1, E]], channel_multiplier=0).then_inc(seen_ok, 1)
            pl.wait_ge(small_in_ok, 64)
            def norm_inverses(n):
                pl.wait_ge(ssv_ok, n + 1)
                wait(pl, r1_ok, n)
                g.tensor_tensor(inv[:, :], ssv[:, :], minus_half[:, :], ALU.pow).then_inc(inv_ok, 1)

            def scales1(n):
                pl.wait_ge(mv1_ok, n + 1)
                g.tensor_tensor(ve1[:, :], mv1[:, :, 1], eps[:, :], ALU.add).then_inc(ve1_ok, 1)
                pl.wait_ge(ve1_ok, n + 1)
                wait(pl, x1_ok, n)
                g.tensor_tensor(rs1[:, :], ve1[:, :], minus_half[:, :], ALU.pow).then_inc(rs1_ok, 1)

            def add_bias(n):
                pl.wait_ge(x1_ok, n + 1)
                g.tensor_tensor(x1b_all[:, 4 * n:4 * n + 4, :], x1[:, n % 2, :, :],
                                bo_all[:, :].unsqueeze(1).broadcast_to([P, 4, D]), ALU.add).then_inc(x1b_ok, 1)

            norm_inverses(0)
            for n in range(NB):
                scales1(n)
                if n + 1 < NB:
                    norm_inverses(n + 1)
                add_bias(n)

            def x1t_copy(p, s):
                wait(pl, s_ready, p - 1)
                src = x1t_all[:, P * p:P * (p + 1)] if isinstance(p, int) else x1t_all[:, bass.ds(p * P, P)]
                g.tensor_copy(x1t[:, s % 2, :], src).then_inc(x1t_ok, 1)

            def rstd(p):
                pl.wait_ge(mv2_ok, p + 1)
                g.tensor_tensor(ve2[:, :], mv2[:, 1:2], eps[:, 0:1], ALU.add).then_inc(ve2_ok, 1)
                pl.wait_ge(ve2_ok, p + 1)
                g.tensor_tensor(rs2[:, :], ve2[:, :], minus_half[:, 0:1], ALU.pow).then_inc(rs2_ok, 1)

            def scatter(p, s):
                if isinstance(p, int) and p == PADDED:
                    pl.wait_ge(pad_ok, 16 * E)
                waits_apart(pl, (row_ok, p + 1), (pos_ok, p + 1))
                at = posi[:, s % 2:s % 2 + 1].bitcast(U32)
                g.indirect_dma_start(out=routed, out_offset=bass.IndirectOffsetOnAxis(ap=at, axis=0),
                                     in_=row[:, s % 2, :], in_offset=None, bounds_check=last_routed,
                                     oob_is_err=False).then_inc(scat_ok[s % 2], 16)

            def slot(p, s, last=False):
                if not (isinstance(p, int) and p == 0):
                    scatter(p - 1, s - 1)
                x1t_copy(p + 2, s)
                rstd(p)

            pl.wait_ge(x1t_all_ok, NB)
            x1t_copy(0, 0)
            x1t_copy(1, 1)
            for s in range(4):
                slot(s, s)
            with pl.Fori(1, NT // 4 - 1) as i:
                for s in range(4):
                    slot(4 * i + s, s)
            slot(NT - 4, 0, last=True)
            slot(NT - 3, 1, last=True)
            rstd(NT - 2)
            scatter(NT - 3, 1)
            rstd(NT - 1)
            scatter(NT - 2, 0)
            scatter(NT - 1, 1)

            def scatter_out(i, u):
                waits_apart(pl, (o3_ok, U * i + u + 1))
                g.indirect_dma_start(out=of,
                                     out_offset=bass.IndirectOffsetOnAxis(ap=token[:, u, :].bitcast(U32), axis=0),
                                     in_=ot[:, u, :], in_offset=None, bounds_check=last_token,
                                     oob_is_err=False).then_inc(out_ok[u], 16)

            def slot(i, u):
                if not (isinstance(i, int) and U * i + u < 2):
                    scatter_out(*back(i, u, 2))
                pl.wait_ge(ve3_ok, U * i + u + 1)
                g.tensor_tensor(rs3[:, u % 3, :], ve3[:, u % 3, :], minus_half[:, 0:1], ALU.pow).then_inc(rs3_ok, 1)

            tiles(pl, slot)
            scatter_out(ROUNDS - 1, LAST - 2)
            scatter_out(ROUNDS - 1, LAST - 1)

        @block.tensor
        def _(pe):
            mm = nc.tensor.matmul
            pe.wait_ge(const_ok, 3)
            pe.wait_ge(key_in_ok, 16)
            for c in range(SC):
                t = nc.tensor.transpose(bank[0][:, P * c:P * (c + 1)], key_in[:, c, :], ident[:, :])
            t.then_inc(keyt_ps, 1)

            def x_transposes(n):
                pe.wait_ge(x_in_ok[n], 16)
                wait(pe, x_lo_ok, n)
                for c in range(4):
                    t = nc.tensor.transpose(bank[1][:, P * c:P * (c + 1)], x_in[:, n, c, :], ident[:, :])
                t.then_inc(xt_ps, 1)

            def scores(n):
                pe.wait_ge(x_hi_ok, n + 1)
                if n == 0:
                    pe.wait_ge(key_hi_ok, 1)
                for c in range(SC):
                    i = SC * n + c
                    wait(pe, gelu_ok, i - 2)
                    o = sc_bank[i % 3]
                    kh, kl = key_hi[:, P * c:P * (c + 1)], key_lo[:, P * c:P * (c + 1)]
                    mm(o, kh, x_hi, start=True, stop=False)
                    if i == 0:
                        pe.wait_ge(key_lo_ok, 1)
                    mm(o, kl, x_hi, start=False, stop=False)
                    if c == 0:
                        pe.wait_ge(x_lo_ok, n + 1)
                    mm(o, kh, x_lo, start=False, stop=True).then_inc(sc_ps, 1)

            def square_sums(n):
                pe.wait_ge(sqsum_ok, 3 * (n + 1))
                wait(pe, ssv_ok, n)
                for t in range(4):
                    m = mm(bank[6][:, t:t + 1], ss_sb[:, n % 2, P * t:P * (t + 1)], ones[:, :], start=True, stop=True)
                m.then_inc(ss_ps, 1)

            def gather(n):
                pe.wait_ge(gelu_ok, SC * (n + 1))
                wait(pe, r1_ok, n - 1)
                if n == 0:
                    pe.wait_ge(value_in_ok, 16)
                for t in range(4):
                    for c in range(SC):
                        m = mm(bank[4 + n % 2][:, P * t:P * (t + 1)], g_sb[:, n % 2, c, P * t:P * (t + 1)],
                               value_in[:, c, :], start=(c == 0), stop=(c == SC - 1))
                m.then_inc(o1_ps, 1)

            def x1_transposes(n):
                pe.wait_ge(x1_ok, n + 1)
                wait(pe, x1t_all_ok, n)
                for c in range(4):
                    t = nc.tensor.transpose(bank[7][:, P * c:P * (c + 1)], x1[:, n % 2, c, :], ident[:, :])
                t.then_inc(x1t_ps, 1)

            x_transposes(0)
            for n in range(NB):
                scores(n)
                if n + 1 < NB:
                    x_transposes(n + 1)
                if n >= 1:
                    square_sums(n - 1)
                    gather(n - 1)
                if n >= 2:
                    x1_transposes(n - 2)
            pe.wait_ge(wqk_in_ok, 32)
            square_sums(NB - 1)
            gather(NB - 1)

            def weight_transposes(i):
                if i == 4:
                    pe.wait_ge(wvo_in_ok, 32)
                if i >= 4:
                    pe.wait_ge(wt_ok, i - 3)
                if i == 0:
                    pe.wait_ge(gelu_ok, SC * NB)
                if i == 1:
                    pe.wait_ge(x_lo_ok, NB)
                w, rows = ((wq_in, P), (wk_in, C), (wv_in, C))[i // 2]
                for c in range(4):
                    at = (4 * (i % 2) + c) * P
                    t = nc.tensor.transpose(bank[i % 4][:, P * c:P * c + rows], w[:, at:at + P], ident[0:rows, 0:rows])
                t.then_inc(wt_ps, 1)

            for i in range(4):
                weight_transposes(i)
            def products(what, i):
                half, h2 = i // 2, i % 2
                o = (a_bank, b_bank)[what][i]
                if what and i < 2:
                    pe.wait_ge(wt_ok, 5 + i)
                elif what and i == 2:
                    pe.wait_ge(ssv_ok, NB)
                elif what:
                    pe.wait_ge(a_lo_ok, 4)
                elif i < 2:
                    pe.wait_ge(gelu_ok, SC * NB)
                else:
                    pe.wait_ge(r1_ok, NB)
                for c in range(4):
                    hp = 4 * half + c
                    rows = slice(DH * h2, DH * (h2 + 1))
                    left = (wkt, wvt)[what][rows, hp, :]
                    right = (wqt, wo_in)[what][rows, hp, :]
                    m = mm(o[0:C, P * c:P * (c + 1)], left, right, start=True, stop=True)
                m.then_inc(ab_ps, 1)

            def ctx_transposes(n, slot, p=None):
                pe.wait_ge(ctx_in_ok[slot], 8 * (n - slot) + 16)
                wait(pe, ctxt_ok, n)
                if p is None:
                    pe.wait_ge(x1t_all_ok, NB - 1)
                else:
                    pe.wait_ge(r2_ok, p + 1)
                for c in range(2):
                    t = nc.tensor.transpose(bank[7][0:C, P * c:P * (c + 1)], ctx_in[:, slot, c, :], ident[:, :])
                t.then_inc(ctxt_ps, 1)

            def group(o, block, q, g):
                if g[1] == KEYS:
                    if g[2] == 0:
                        pe.wait_ge(ctxt_lo_ok, block + 1)
                    for c in range(2):
                        ah, al = a_hi[:, c, g[2], :], a_lo[:, c, g[2], :]
                        half = o[:, 256 * c:256 * (c + 1)]
                        mm(half, ah, ctxt_hi[:, q, :], start=True, stop=False)
                        mm(half, ah, ctxt_lo[:, q, :], start=False, stop=False)
                        m = mm(half, al, ctxt_hi[:, q, :], start=False, stop=True)
                else:
                    pair, four = g[2] // 4, g[2] % 4
                    hi, lo = ctxt_hi[:, q, P * pair:P * (pair + 1)], ctxt_lo[:, q, P * pair:P * (pair + 1)]
                    bh, bl = b_hi[:, :, 2 * four:2 * four + 2, :], b_lo[:, :, 2 * four:2 * four + 2, :]
                    o = o.rearrange("p (a c d) -> p a c d", a=2, c=2)
                    mm(o, hi, bh, start=True, stop=False)
                    mm(o, hi, bl, start=False, stop=False)
                    m = mm(o, lo, bh, start=False, stop=True)
                m.then_inc(kz_ps, 1)

            def group_left(p, s, was, last):
                before = opening[-8:] if isinstance(p, int) and p == 0 else [g for _, g in places(s + 1, False)]
                both = before + [g for _, g in places(s, last)]
                wait(pe, kz_ok, OPEN + 8 * p + was + 1)
                if shared(both[8 + was]):
                    wait(pe, z_ok, SHARED + 2 * p + sum(map(shared, both[:8 + was + 1])) - sum(map(shared, before)))

            def slot_group(p, s, n, at, g, last):
                if GROUP_BEFORE[at] is not None:
                    group_left(p, s, GROUP_BEFORE[at], last)
                group(kz_of(at), n + g[0], (s // 2 + g[0]) % 2, g)

            def opening_group(n):
                g, was = opening[n], n - 5
                if was >= 0:
                    wait(pe, kz_ok, was + 1)
                    if shared(opening[was]):
                        wait(pe, z_ok, sum(map(shared, opening[:was + 1])))
                elif n < 3:
                    pe.wait_ge(a_lo_ok, n + 1)
                else:
                    pe.wait_ge(b_lo_ok, 4)
                group(ring[n % 5], g[0], g[0], g)

            def cross_scores(p, s):
                q, j = s // 2 % 2, s % 2
                pe.wait_ge(x1t_ok, p + 1)
                wait(pe, sub_ok, p)
                pe.wait_ge(kz_ok, 8 if isinstance(p, int) and p == 0
                           else OPEN + 8 * (p - j - 2) + even.index((1, KEYS, 7)) + 1)
                for half in range(2):
                    for b in range(2):
                        at = P * j + L * b
                        m = mm(bank[half][L * b:L * (b + 1), :].rearrange("q (h k) -> q h k", k=L),
                               x1t[:, s % 2, L * b:L * (b + 1)], kp_all[:, q, 8 * half:8 * half + 8, at:at + L],
                               start=True, stop=True)
                m.then_inc(s_ready, 1)

            def prob_transposes(p, s, last):
                pe.wait_ge(pn_ok, p + 1)
                for half in range(2):
                    if not (last and s >= 2):
                        group_left(p, s, HALF_BEFORE[half], last)
                    for c in range(HP // 2):
                        at = HP * half + 2 * c
                        t = nc.tensor.transpose(HALVES[half][:, P * c:P * (c + 1)],
                                                pn_sb[:, at:at + 2, :].rearrange("p a k -> p (a k)"), ident[:, :])
                    t.then_inc(pt_ready, 1)

            def attend(p, s):
                q, j = s // 2 % 2, s % 2
                o = o2_of(p)
                if not (isinstance(p, int) and p >= NT - 2):
                    wait(pe, place_ok, p)
                if isinstance(p, int) and p == PADDED:
                    pe.wait_ge(pad_at_ok, 1)
                if isinstance(p, int) and p < 2:
                    pe.wait_ge(kz_ok, OPEN)
                else:
                    pe.wait_ge(kz_ok, GROUPS if isinstance(p, int) and p == NT - 1 else OPEN + 8 * (p - 1) - j)
                pe.wait_ge(z_ok, 2 * p + 2)
                if isinstance(p, int) and p == NT - 2:
                    group_left(NT - 3, 1, 1, last=True)
                for c in range(HP):
                    if c % (HP // 2) == 0:
                        pe.wait_ge(pt_ok, 2 * p + 2 * c // HP + 1)
                    for b in range(2):
                        m = mm(o[L * b:L * (b + 1), :], pt_sb[:, c, L * b:L * (b + 1)],
                               z_all[:, q, j, b, c, :], start=(c == 0), stop=(c == HP - 1))
                m.then_inc(o2_ps, 1)

            def x2_transpose(p, j, has_ctx):
                pe.wait_ge(x2_ok, p + 1)
                if has_ctx is not None:
                    pe.wait_ge(ctxt_ok, has_ctx + 1)
                nc.tensor.transpose(bank[7][:, 0:P], row[:, j, 0:D], ident[:, :]).then_inc(x2t_ps, 1)

            def router_logits(p):
                pe.wait_ge(x2t_ok, p + 1)
                mm(lg_bank, x2t[:, :], wr_sb[:, :], start=True, stop=True).then_inc(lg_ps, 1)

            def ranks(p):
                pe.wait_ge(oh_ok, p + 1)
                wait(pe, seen_up, p)
                o = rank_bank
                mm(o, before_b[:, :], oh_b[:, :], start=True, stop=False)
                mm(o, ones_b[:, :], seen_b[:, :], start=False, stop=True).then_inc(rank_ps, 1)

            def expert_counts(pairs):
                pe.wait_ge(seen_up, pairs)
                mm(rank_bank, ones_b[:, :], seen_b[:, :], start=True, stop=True).then_inc(count_ps, 1)

            def slot(p, s, n, last=False):
                j = s % 2

                def kz(*at):
                    for place, g in places(s, last):
                        if place in at and not (last and s == 1 and place >= 2):
                            slot_group(p, s, n, place, g, last)

                cross_scores(p + 1, s + 1)
                kz(0)
                if not (isinstance(p, int) and p == 0):
                    ranks(p - 1)
                prob_transposes(p, s, last)
                if isinstance(p, int) and p == PADDED:
                    expert_counts(PADDED)
                kz(1, 2)
                attend(p, s)
                kz(3)
                has_ctx = j == 0 and not last
                if has_ctx:
                    ctx_transposes(n + 2, (s // 2) % 2, p)
                kz(4, 5, 6)
                if last and s == 1:
                    cross_scores(NT - 1, 3)
                x2_transpose(p, j, n + 2 if has_ctx else None)
                kz(7)
                router_logits(p)

            x1_transposes(NB - 2)
            weight_transposes(4)
            weight_transposes(5)
            pe.wait_ge(wt_ok, 4)
            for i in range(4):
                products(0, i)
            ctx_transposes(0, 0)
            pe.wait_ge(wt_ok, 6)
            products(1, 0)
            products(1, 1)
            products(1, 2)
            ctx_transposes(1, 1)
            products(1, 3)
            pe.wait_ge(small_in_ok, 64)
            pe.wait_ge(b_lo_ok, 1)
            nc.tensor.transpose(bank[0][:, 0:E * FC], b1_in[:, :], ident[0:E * FC, 0:E * FC]).then_inc(b1t_ps, 1)
            pe.wait_ge(ctxt_ok, 2)
            x1_transposes(NB - 1)
            for n in range(9):
                opening_group(n)
            cross_scores(0, 0)
            for n in range(9, OPEN):
                opening_group(n)
            for s in range(4):
                slot(s, s, s // 2)
            with pe.Fori(1, NT // 4 - 1) as i:
                for s in range(4):
                    slot(4 * i + s, s, 2 * i + s // 2)
            slot(NT - 4, 0, NT // 2 - 2, last=True)
            slot(NT - 3, 1, NT // 2 - 2, last=True)
            prob_transposes(NT - 2, 2, last=True)
            attend(NT - 2, 2)
            ranks(NT - 3)
            for place, g in places(1, True)[2:]:
                slot_group(NT - 3, 1, NT // 2 - 2, place, g, last=True)
            prob_transposes(NT - 1, 3, last=True)
            attend(NT - 1, 3)
            x2_transpose(NT - 2, 0, None)
            router_logits(NT - 2)
            ranks(NT - 2)
            pe.wait_ge(place_ok, NT - 1)
            x2_transpose(NT - 1, 1, None)
            router_logits(NT - 1)
            ranks(NT - 1)
            expert_counts(NT)

            def transpose_rows(i, u):
                pe.wait_ge(xs_ok[u], 16 * (i + 1))
                nc.tensor.transpose(bank[u % 2][:, 0:P], xs[:, u, 0:D], ident[:, :]).then_inc(xst_ps, 1)

            def hidden(i, u):
                t = U * i + u
                pe.wait_ge(ew_ok, t + 1)
                pe.wait_ge(xst_ok, t + 1)
                for c in range(FC):
                    m = mm(bank[2 + u % 2][:, P * c:P * (c + 1)], ew[:, u, P * c:P * (c + 1)], xst[:, u % 2, :],
                           start=True, stop=True)
                m.then_inc(h_ps, 1)

            def project(i, u, e):
                t = U * i + u
                pe.wait_ge(h_ok, FC * (t + 1))
                wait(pe, yb_ok, t - 1)
                for c in range(FC):
                    m = mm(bank[4 + u % 2][:, 0:D], ht[:, u % 2, c, :], w2_all[:, bass.ds(e, 1), c, :],
                           start=(c == 0), stop=(c == FC - 1))
                m.then_inc(y_ps, 1)

            def slot(i, u):
                e = pe.value_load(expert_of[0:1, bass.ds(U * i + u, 1)], min_val=0, max_val=E - 1)
                if ahead(i, u, 2):
                    transpose_rows(*ahead(i, u, 2))
                if ahead(i, u, 1):
                    hidden(*ahead(i, u, 1))
                project(i, u, e)

            pe.wait_ge(table_ok, 1)
            pe.wait_ge(experts_in_ok, 48)
            transpose_rows(0, 0)
            transpose_rows(0, 1)
            hidden(0, 0)
            tiles(pe, slot)

        @block.scalar
        def _(act):
            a = nc.scalar.activation
            def split_x(n):
                act.wait_ge(xt_ps, n + 1)
                wait(act, sc_ps, SC * n)
                a(x_hi, bank[1], ACT.Copy).then_inc(x_hi_ok, 1)

            def gelu(n, c):
                i = SC * n + c
                act.wait_ge(sc_ps, i + 1)
                if c == 0:
                    wait(act, o1_ps, n - 1)
                a(g_sb[:, n % 2, c, :], sc_bank[i % 3], ACT.Gelu).then_inc(gelu_ok, 1)

            def square(n, c):
                act.wait_ge(gelu_ok, SC * n + c + 1)
                wait(act, sqsum_ok, 3 * n)
                a(sq_sb[:, c, :], g_sb[:, n % 2, c, :], ACT.Square).then_inc(sq_ok, 1)

            def x1t_copy(n):
                act.wait_ge(x1t_ps, n + 1)
                a(x1t_all[:, 512 * n:512 * (n + 1)], bank[7], ACT.Copy).then_inc(x1t_all_ok, 1)

            act.wait_ge(seen_ok, 5)
            a(table_in[:, :], eps[:, 0:1], ACT.Gelu)
            split_x(0)
            for n in range(NB):
                for c in range(SC):
                    gelu(n, c)
                    if 1 <= c < 3:
                        square(n, c - 1)
                if n + 1 < NB:
                    split_x(n + 1)
                square(n, 2)
                square(n, 3)
                if n >= 2:
                    x1t_copy(n - 2)
            for i in range(6):
                act.wait_ge(wt_ps, i + 1)
                dst, rows = ((wqt, P), (wkt, C), (wvt, C))[i // 2]
                a(dst[:, 4 * (i % 2):4 * (i % 2) + 4, :],
                  bank[i % 4].rearrange("p (c n) -> p c n", n=P)[:, :, 0:rows], ACT.Copy).then_inc(wt_ok, 1)
                if i == 3:
                    x1t_copy(NB - 2)
            def ab_copy(i):
                act.wait_ge(ab_ps, i + 1)
                half, h2 = i // 2 % 2, i % 2
                src = (a_bank + list(b_bank))[i][0:C, :].rearrange("c (a d) -> c a d", d=D)
                if i < 4:
                    a(a_hi[:, h2, 4 * half:4 * half + 4, :], src, ACT.Copy).then_inc(a_hi_ok, 1)
                else:
                    a(b_hi[:, h2, 4 * half:4 * half + 4, :], src, ACT.Copy).then_inc(b_ok, 1)

            def ctx_copy(n, slot):
                act.wait_ge(ctxt_ps, n + 1)
                a(ctxt[:, slot, :], bank[7][0:C, 0:256], ACT.Copy).then_inc(ctxt_ok, 1)

            for i in range(4):
                ab_copy(i)
            a(table_in[:, :], eps[:, 0:1], ACT.Exp)
            ctx_copy(0, 0)
            ab_copy(4)
            ab_copy(5)
            ctx_copy(1, 1)
            ab_copy(6)
            ab_copy(7)
            act.wait_ge(b1t_ps, 1)
            a(ew_all[:, :, F:F + FC], bank[0][:, 0:E * FC].rearrange("p (e c) -> p e c", c=FC), ACT.Copy
              ).then_inc(b1t_ok, 1)
            x1t_copy(NB - 1)

            def kz_copy(n, bank, q, g):
                act.wait_ge(kz_ps, n + 1)
                if g[1] == KEYS:
                    m = a(kp_all[:, q, 2 * g[2]:2 * g[2] + 2, :], bank.rearrange("p (c t) -> p c t", t=256),
                          ACT.Copy)
                else:
                    for b in ((1,) if shared(g) else (0, 1)):
                        for h2 in range(2):
                            m = z_copy(a, bank, q, g, b, h2, ACT.Copy)
                m.then_inc(kz_ok, 1)

            def exps(p):
                act.wait_ge(sub_ok, p + 1)
                wait(act, pn_ok, p)
                a(pe_sb[:, :, :], ps_sb[:, :, :], ACT.Exp, scale=SCALE).then_inc(exp_ok, 1)

            def gate_exp(p):
                act.wait_ge(ld_ok, p + 1)
                wait(act, row_ok, p)
                a(lexp[:, :], ld[:, :], ACT.Exp, accum_out=lsum[:, :]).then_inc(lsum_ok, 1)

            def prob_copy(p):
                for half in range(2):
                    act.wait_ge(pt_ready, 2 * p + half + 1)
                    a(pt_sb[:, HP // 2 * half:HP // 2 * (half + 1), :],
                      HALVES[half].rearrange("p (c q) -> p c q", q=P), ACT.Copy).then_inc(pt_ok, 1)

            def x2t_copy(p):
                act.wait_ge(x2t_ps, p + 1)
                a(x2t[:, :], bank[7][:, 0:P], ACT.Copy).then_inc(x2t_ok, 1)

            def slot(p, s, n, last=False):
                def kz(*at):
                    for place, g in places(s, last):
                        if place in at and not (last and s == 1 and place >= 2):
                            kz_copy(OPEN + 8 * p + place, kz_of(place), (s // 2 + g[0]) % 2, g)

                if not (isinstance(p, int) and p == 0):
                    gate_exp(p - 1)
                kz(0)
                prob_copy(p)
                exps(p + 1)
                kz(1, 2, 3)
                if s % 2 == 0 and not last:
                    ctx_copy(n + 2, (s // 2) % 2)
                kz(4, 5)
                x2t_copy(p)
                kz(6, 7)

            for n, g in enumerate(opening):
                if n == 13:
                    exps(0)
                kz_copy(n, ring[n % 5], g[0], g)
            for s in range(4):
                slot(s, s, s // 2)
            with act.Fori(1, NT // 4 - 1) as i:
                for s in range(4):
                    slot(4 * i + s, s, 2 * i + s // 2)
            slot(NT - 4, 0, NT // 2 - 2, last=True)
            slot(NT - 3, 1, NT // 2 - 2, last=True)
            prob_copy(NT - 2)
            exps(NT - 1)
            gate_exp(NT - 3)
            for place, g in places(1, True)[2:]:
                kz_copy(OPEN + 8 * (NT - 3) + place, kz_of(place), (NT // 2 - 1) % 2, g)
            prob_copy(NT - 1)
            x2t_copy(NT - 2)
            gate_exp(NT - 2)
            x2t_copy(NT - 1)
            gate_exp(NT - 1)

            def transposed_copy(i, u):
                t = U * i + u
                act.wait_ge(xst_ps, t + 1)
                wait(act, h_ps, t - 1)
                a(xst[:, u % 2, :], bank[u % 2][:, 0:P], ACT.Copy).then_inc(xst_ok, 1)

            def gelus(i, u):
                t = U * i + u
                act.wait_ge(h_ps, t + 1)
                wait(act, y_ps, t - 1)
                for c in range(FC):
                    a(ht[:, u % 2, c, :], bank[2 + u % 2][:, P * c:P * (c + 1)], ACT.Gelu,
                      bias=ew[:, u, F + c:F + c + 1]).then_inc(h_ok, 1)

            def slot(i, u):
                if ahead(i, u, 2):
                    transposed_copy(*ahead(i, u, 2))
                if ahead(i, u, 1):
                    gelus(*ahead(i, u, 1))

            a(table_in[:, :], eps[:, 0:1], ACT.Gelu)
            transposed_copy(0, 0)
            transposed_copy(0, 1)
            gelus(0, 0)
            tiles(act, slot)

        @block.vector
        def _(dve):
            v = nc.vector
            dve.wait_ge(keyt_ps, 1)
            v.tensor_copy(key_hi, bank[0]).then_inc(key_hi_ok, 1)
            dve.wait_ge(key_hi_ok, 1)
            v.tensor_tensor(key_lo, bank[0], key_hi.bitcast(F32), ALU.subtract).then_inc(key_lo_ok, 1)

            def split_x(n):
                dve.wait_ge(x_hi_ok, n + 1)
                wait(dve, sc_ps, SC * n)
                v.tensor_tensor(x_lo, bank[1], x_hi.bitcast(F32), ALU.subtract).then_inc(x_lo_ok, 1)

            def mean_squares(n):
                dve.wait_ge(ss_ps, n + 1)
                wait(dve, inv_ok, n)
                v.tensor_scalar(ssv[:, :], bank[6][:, 0:4], 1.0 / S, None, ALU.mult).then_inc(ssv_ok, 1)

            def stats1(n):
                dve.wait_ge(inv_ok, n + 1)
                dve.wait_ge(o1_ps, n + 1)
                wait(dve, x1_ok, n)
                for t in range(4):
                    m = v.scalar_tensor_tensor(r1[:, t, :], bank[4 + n % 2][:, P * t:P * (t + 1)], inv[:, t:t + 1],
                                               x_in[:, n, t, :], ALU.mult, ALU.add)
                m.then_inc(r1_ok, 1)
                dve.wait_ge(r1_ok, n + 1)
                for t in range(4):
                    m = v.bn_stats(st1[:, t, :], r1[:, t, :])
                m.then_inc(st1_ok, 1)
                dve.wait_ge(st1_ok, n + 1)
                wait(dve, ve1_ok, n)
                for t in range(4):
                    m = v.bn_aggr(mv1[:, t, :], st1[:, t, :])
                m.then_inc(mv1_ok, 1)

            def norm1(n):
                dve.wait_ge(rs1_ok, n + 1)
                wait(dve, x1t_ps, n - 1)
                wait(dve, x1b_ok, n - 1)
                for t in range(4):
                    m = v.tensor_scalar(x1[:, n % 2, t, :], r1[:, t, :], mv1[:, t, 0:1], rs1[:, t:t + 1],
                                        ALU.subtract, ALU.mult)
                m.then_inc(x1_ok, 1)

            def add_squares(n, step):
                if step < 2:
                    dve.wait_ge(sq_ok, SC * n + 2 * step + 2)
                    v.tensor_tensor(sq2[:, step, :], sq_sb[:, 2 * step, :], sq_sb[:, 2 * step + 1, :], ALU.add
                                    ).then_inc(sqsum_ok, 1)
                else:
                    dve.wait_ge(sqsum_ok, 3 * n + 2)
                    wait(dve, ss_ps, n - 1)
                    v.tensor_tensor(ss_sb[:, n % 2, :], sq2[:, 0, :], sq2[:, 1, :], ALU.add).then_inc(sqsum_ok, 1)

            split_x(0)
            for n in range(NB):
                if n >= 2:
                    stats1(n - 2)
                add_squares(n, 0)
                if n >= 2:
                    norm1(n - 2)
                if n + 1 < NB:
                    split_x(n + 1)
                add_squares(n, 1)
                add_squares(n, 2)
                if n >= 1:
                    mean_squares(n - 1)
            stats1(NB - 2)
            mean_squares(NB - 1)
            norm1(NB - 2)
            stats1(NB - 1)

            def a_low(i):
                dve.wait_ge(a_hi_ok, i + 1)
                half, h2 = i // 2, i % 2
                v.tensor_tensor(a_lo[:, h2, 4 * half:4 * half + 4, :],
                                a_bank[i][0:C, :].rearrange("c (a d) -> c a d", d=D),
                                a_hi[:, h2, 4 * half:4 * half + 4, :].bitcast(F32), ALU.subtract).then_inc(a_lo_ok, 1)

            a_low(0)
            norm1(NB - 1)
            for i in range(1, 4):
                a_low(i)

            def split_ctx(n, slot):
                dve.wait_ge(ctxt_ok, n + 1)
                if not (isinstance(n, int) and n < 2):
                    dve.wait_ge(kz_ps, OPEN + 8 * (2 * n - 5) + 7)
                v.tensor_copy(ctxt_hi[:, slot, :], ctxt[:, slot, :]).then_inc(ctxt_hi_ok, 1)
                dve.wait_ge(ctxt_hi_ok, n + 1)
                v.tensor_tensor(ctxt_lo[:, slot, :], ctxt[:, slot, :], ctxt_hi[:, slot, :].bitcast(F32), ALU.subtract
                                ).then_inc(ctxt_lo_ok, 1)

            for i in range(4):
                if i % 2 == 0:
                    split_ctx(i // 2, i // 2)
                dve.wait_ge(b_ok, i + 1)
                half, h2 = i // 2, i % 2
                v.tensor_tensor(b_lo[:, h2, 4 * half:4 * half + 4, :],
                                b_bank[i][0:C, :].rearrange("c (a d) -> c a d", d=D),
                                b_hi[:, h2, 4 * half:4 * half + 4, :].bitcast(F32), ALU.subtract).then_inc(b_lo_ok, 1)

            def z_part(n, bank, q, g):
                dve.wait_ge(kz_ps, n + 1)
                z_copy(v.tensor_copy, bank, q, g, 0, 0)
                z_copy(v.tensor_copy, bank, q, g, 0, 1).then_inc(z_ok, 1)

            def heads(t):
                return t[:, :].unsqueeze(2).broadcast_to([P, H, L])

            def maxes(p):
                dve.wait_ge(s_ready, p + 1)
                v.reduce_max(smax[:, :], s_ps, AX.X).then_inc(max_ok, 1)

            def subtract_max(p):
                dve.wait_ge(max_ok, p + 1)
                wait(dve, exp_ok, p)
                v.tensor_tensor(ps_sb[:, :, :], s_ps, heads(smax), ALU.subtract).then_inc(sub_ok, 1)

            def sums(p):
                dve.wait_ge(exp_ok, p + 1)
                v.reduce_sum(prob_sum[:, :], pe_sb[:, :, :], AX.X).then_inc(sum_ok, 1)

            def reciprocals(p):
                dve.wait_ge(sum_ok, p + 1)
                v.reciprocal(pinv[:, :], prob_sum[:, :]).then_inc(pinv_ok, 1)

            def normalise(p):
                dve.wait_ge(pinv_ok, p + 1)
                wait(dve, pt_ready, 2 * p)
                v.tensor_tensor(pn_sb[:, :, :], pe_sb[:, :, :], heads(pinv), ALU.mult).then_inc(pn_ok, 1)

            def at(tensor, p):
                return tensor[:, p, :] if isinstance(p, int) else tensor[:, bass.ds(p, 1), :]

            def add_x1(p):
                dve.wait_ge(o2_ps, p + 1)
                v.tensor_tensor(r2[:, :], o2_of(p), at(x1b_all, p), ALU.add).then_inc(r2_ok, 1)

            def stats2(p):
                dve.wait_ge(r2_ok, p + 1)
                v.bn_stats(st2[:, :], r2[:, :]).then_inc(st2_ok, 1)
                waits_apart(dve, (x2_ok, p), (st2_ok, p + 1))
                v.bn_aggr(mv2[:, :], st2[:, :]).then_inc(mv2_ok, 1)

            def norm2(p, s):
                dve.wait_ge(rs2_ok, p + 1)
                if not (isinstance(p, int) and p < 2):
                    dve.wait_ge(scat_ok[s % 2], 8 * (p - s % 2))
                v.tensor_scalar(row[:, s % 2, 0:D], r2[:, :], mv2[:, 0:1], rs2[:, :], ALU.subtract, ALU.mult
                                ).then_inc(x2_ok, 1)

            def choose(p):
                dve.wait_ge(lg_ps, p + 1)
                v.tensor_tensor(lg[:, :], lg_bank, br_all[:, :], ALU.add).then_inc(lg_ok, 1)
                waits_apart(dve, (lg_ok, p + 1))
                v.max(lmax[:, :], lg[:, :]).then_inc(lmax_ok, 1)
                waits_apart(dve, (lmax_ok, p + 1))
                v.max_index(lidx[:, :], lmax[:, :], lg[:, :]).then_inc(lidx_ok, 1)
                v.tensor_scalar(ld[:, :], lg[:, :], lmax[:, 0:1], None, ALU.subtract).then_inc(ld_ok, 1)
                dve.wait_ge(lidx_ok, p + 1)
                v.tensor_copy(lidf[:, :], lidx[:, 0:1]).then_inc(lidf_ok, 1)
                dve.wait_ge(lidf_ok, p + 1)
                wait(dve, rank_ps, p)
                v.tensor_scalar(oh_b[:, :], expert_no[:, :], lidf[:, :], None, ALU.is_equal).then_inc(oh_ok, 1)

            def read_ranks(p):
                dve.wait_ge(rank_ps, p + 1)
                v.tensor_tensor(place[:, :], rank_bank, region_base[:, :], ALU.add).then_inc(place_ok, 1)
                v.tensor_tensor(seen_b[:, :], seen_b[:, :], oh_b[:, :], ALU.add).then_inc(seen_up, 1)

            def finish_row(p, s):
                dve.wait_ge(place_ok, p + 1)
                v.tensor_tensor(placed[:, :], place[:, :], oh_b[:, :], ALU.mult).then_inc(placed_ok, 1)
                src = token_no[:, p:p + 1] if isinstance(p, int) else token_no[:, bass.ds(p, 1)]
                v.tensor_copy(row[:, s % 2, TOKEN:TOKEN + 1].bitcast(I32), src)
                dve.wait_ge(placed_ok, p + 1)
                v.reduce_sum(posf[:, :], placed[:, :], AX.X).then_inc(placed2, 1)
                dve.wait_ge(lsum_ok, p + 1)
                v.reciprocal(row[:, s % 2, GATE:GATE + 1], lsum[:, :]).then_inc(row_ok, 1)
                dve.wait_ge(placed2, p + 1)
                v.tensor_copy(posi[:, s % 2:s % 2 + 1], posf[:, :]).then_inc(pos_ok, 1)

            def slot(p, s, n, last=False):
                first = isinstance(p, int) and p == 0

                def z_at(which):
                    mine = [(at, g) for at, g in places(s, last) if shared(g)]
                    if mine:
                        at, g = mine[which]
                        z_part(OPEN + 8 * p + at, kz_of(at), (s // 2 + g[0]) % 2, g)

                maxes(p + 1)
                if not first:
                    read_ranks(p - 1)
                subtract_max(p + 1)
                if isinstance(p, int) and p == PADDED:
                    dve.wait_ge(count_ps, 1)
                    v.tensor_tensor(pad_at[:, :], rank_bank[0:1, :], region_base[0:1, :], ALU.add
                                    ).then_inc(pad_at_ok, 1)
                z_at(0)
                if not first:
                    finish_row(p - 1, (s - 1) % 2)
                sums(p + 1)
                add_x1(p)
                reciprocals(p + 1)
                stats2(p)
                if s % 2 == 1:
                    z_at(1)
                norm2(p, s)
                normalise(p + 1)
                if s % 2 == 0:
                    z_at(1)
                if s % 2 == 0 and not last:
                    split_ctx(n + 2, (s // 2) % 2)
                if last and s == 1:
                    maxes(NT - 1)
                    subtract_max(NT - 1)
                choose(p)

            mine = [n for n, g in enumerate(opening) if shared(g)]

            def opening_part(i):
                z_part(mine[i], ring[mine[i] % 5], 0, opening[mine[i]])

            opening_part(0)
            maxes(0)
            subtract_max(0)
            opening_part(1)
            sums(0)
            opening_part(2)
            reciprocals(0)
            normalise(0)
            opening_part(3)
            for s in range(4):
                slot(s, s, s // 2)
            with dve.Fori(1, NT // 4 - 1) as i:
                for s in range(4):
                    slot(4 * i + s, s, 2 * i + s // 2)
            slot(NT - 4, 0, NT // 2 - 2, last=True)
            slot(NT - 3, 1, NT // 2 - 2, last=True)
            sums(NT - 1)
            read_ranks(NT - 3)
            reciprocals(NT - 1)
            normalise(NT - 1)
            add_x1(NT - 2)
            stats2(NT - 2)
            finish_row(NT - 3, 1)
            norm2(NT - 2, 2)
            dve.wait_ge(x2_ok, NT - 1)
            add_x1(NT - 1)
            stats2(NT - 1)
            choose(NT - 2)
            norm2(NT - 1, 3)
            read_ranks(NT - 2)
            finish_row(NT - 2, 0)
            choose(NT - 1)
            read_ranks(NT - 1)
            finish_row(NT - 1, 1)

            steps = [0]

            def step(ins):
                steps[0] += 1
                ins.then_inc(tab, 1)
                dve.wait_ge(tab, steps[0])

            dve.wait_ge(count_ps, 2)
            dve.wait_ge(seen_ok, 6)
            counts = rank_bank[0:1, :]
            step(v.tensor_scalar(n_int[:, :], counts, float(P - 1), None, ALU.add))
            step(v.tensor_scalar(n_tiles[:, :], n_int[:, :], 7, None, ALU.logical_shift_right))
            step(v.tensor_scalar(tl_skip[:, :], n_tiles[:, :], -float(P), float(REGION), ALU.mult, ALU.add))
            step(v.tensor_tensor(tl_mul[:, :, :], n_tiles[:, :].unsqueeze(1).broadcast_to([1, E, E]),
                                 le_expert[:, :, :], ALU.mult))
            step(v.reduce_sum(tl_end[:, :], tl_mul[:, :, :], AX.X))
            wide = [1, TILES, E]
            step(v.tensor_tensor(past[:, :, :], tl_end[:, :].unsqueeze(1).broadcast_to(wide), tile_no[:, :, :],
                                 ALU.is_le))
            step(v.reduce_sum(past_n[:, :], past[:, :, :], AX.X))
            step(v.tensor_scalar(expert_of[:, :], past_n[:, :], float(E - 1), None, ALU.min))
            step(v.tensor_tensor(skip[:, :, :], past[:, :, :], tl_skip[:, :].unsqueeze(1).broadcast_to(wide),
                                 ALU.mult))
            step(v.reduce_sum(skip_n[:, :], skip[:, :, :], AX.X))
            v.tensor_tensor(row_of[:, :], skip_n[:, :], tile_row[:, :], ALU.add).then_inc(table_ok, 1)
            dve.wait_ge(table_ok, 1)
            dve.wait_ge(experts_in_ok, 48)
            dve.wait_ge(b1t_ok, 1)

            def expert_load(i, u):
                return dve.value_load(expert_of[0:1, bass.ds(U * i + u, 1)], min_val=0, max_val=E - 1)

            def expert_copy(i, u, e):
                wait(dve, h_ok, FC * (U * i + u - U + 1))
                v.tensor_copy(ew[:, u, :], ew_all[:, bass.ds(e, 1), :]).then_inc(ew_ok, 1)

            def scales3(i, u):
                waits_apart(dve, (st3_ok, U * i + u + 1))
                v.bn_aggr(mv3[:, u % 3, :], st3[:, u % 3, :]).then_inc(mv3_ok, 1)

            def add_eps3(i, u):
                dve.wait_ge(mv3_ok, U * i + u + 1)
                v.tensor_tensor(ve3[:, u % 3, :], mv3[:, u % 3, 1:2], eps[:, 0:1], ALU.add).then_inc(ve3_ok, 1)

            def norm3(i, u):
                dve.wait_ge(rs3_ok, U * i + u + 1)
                v.tensor_scalar(ot[:, u, :], r3[:, u % 3, :], mv3[:, u % 3, 0:1], rs3[:, u % 3, :],
                                ALU.subtract, ALU.mult).then_inc(o3_ok, 1)

            def slot(i, u):
                t, b = U * i + u, u % 2
                after = ahead(i, u, 4)
                if after:
                    e = expert_load(*after)
                dve.wait_ge(y_ps, t + 1)
                v.tensor_tensor(yb[:, b, :], bank[4 + b][:, 0:D], ew[:, u, F + FC:EW], ALU.add).then_inc(yb_ok, 1)
                if not (isinstance(i, int) and t < 1):
                    scales3(*back(i, u, 1))
                if after:
                    expert_copy(*after, e)
                if not (isinstance(i, int) and t < 1):
                    add_eps3(*back(i, u, 1))
                dve.wait_ge(yb_ok, t + 1)
                v.scalar_tensor_tensor(r3[:, u % 3, :], yb[:, b, :], xs[:, u, GATE:GATE + 1], xs[:, u, 0:D],
                                       ALU.mult, ALU.add).then_inc(r3_ok, 1)
                if not (isinstance(i, int) and i == 0):
                    dve.wait_ge(out_ok[u], 16 * i)
                v.tensor_copy(token[:, u, :], xs[:, u, TOKEN:TOKEN + 1]).then_inc(token_ok, 1)
                if not (isinstance(i, int) and t < 2):
                    norm3(*back(i, u, 2))
                dve.wait_ge(r3_ok, t + 1)
                v.bn_stats(st3[:, u % 3, :], r3[:, u % 3, :]).then_inc(st3_ok, 1)

            for u in range(4):
                expert_copy(0, u, expert_load(0, u))
            tiles(dve, slot)
            scales3(ROUNDS - 1, LAST - 1)
            add_eps3(ROUNDS - 1, LAST - 1)
            norm3(ROUNDS - 1, LAST - 2)
            norm3(ROUNDS - 1, LAST - 1)


_INS = ["x", "ctx_768", "L0_attn_key_param_tokens", "L0_attn_value_param_tokens", "L0_xattn_Wq", "L0_xattn_Wk",
        "L0_xattn_Wv", "L0_xattn_Wo", "L0_xattn_bo", "L0_ffn_W1", "L0_ffn_b1", "L0_ffn_W2", "L0_ffn_b2",
        "L0_ffn_Wr", "L0_ffn_br"]


def kernel(**inputs):
    import numpy as np
    import concourse.bacc as bacc
    from concourse import mybir as mb
    from concourse.bass_utils import run_bass_kernel_spmd

    nc = bacc.Bacc("TRN2", target_bir_lowering=False, num_devices=1)
    arrays, args = {}, []
    for name in _INS:
        a = np.ascontiguousarray(inputs[name])
        arrays[f"in_{name}"] = a
        args.append(nc.dram_tensor(f"in_{name}", a.shape, mb.dt.from_np(a.dtype), kind="ExternalInput").ap())
    args.append(nc.dram_tensor("out", (32, 64, 128), mb.dt.float32, kind="ExternalOutput").ap())
    build_program(nc, *args)
    r = run_bass_kernel_spmd(nc, [arrays], core_ids=[0])
    return r.results[0]["out"]
```
